# Optimizing a Trainium2 kernel written in Bass

```python
import numpy as np
import jax
import jax.numpy as jnp

def _softmax(x, axis=-1):
    return jax.nn.softmax(x, axis=axis)

def _gelu(x):
    return jax.nn.gelu(x, approximate=True)

def _silu(x):
    return jax.nn.silu(x)

def _sigmoid(x):
    return jax.nn.sigmoid(x)

def _layernorm(x, axis=-1, eps=1e-05):
    m = jnp.mean(x, axis=axis, keepdims=True)
    v = jnp.var(x, axis=axis, keepdims=True)
    return (x - m) / jnp.sqrt(v + eps)

def _scatter_add(tgt, idx, src, axis=0):
    return tgt.at[idx].add(src)

def _segment_sum(src, seg, n):
    return jax.ops.segment_sum(src, seg, n)
kernel_name = 'mk_prb_d1_jaxref_r8_8adad0'

def setup_inputs(seed: int=0):
    np.random.seed(seed)
    _w = jnp.asarray

    def _L0_attn_setup():
        import jax, jax.numpy as jnp
        import numpy as np
        D_MODEL = 256
        H = 16
        HKV = 4
        DS = 32
        DG = 32
        DV = 64
        B, T = (2, 512)
        MB = 64
        LW = 128
        ROPE_BASE = 10000.0
        NEG_INF = -1000000000.0

        def _rope(x, pos, base):
            d = x.shape[-1]
            inv_freq = 1.0 / base ** (jnp.arange(0, d, 2, dtype=jnp.float32) / d)
            ang = pos.astype(jnp.float32)[:, None] * inv_freq
            cos, sin = (jnp.cos(ang), jnp.sin(ang))
            x1, x2 = jnp.split(x, 2, axis=-1)
            return jnp.concatenate([x1 * cos - x2 * sin, x2 * cos + x1 * sin], axis=-1)
        key = jax.random.key(seed)
        ks = jax.random.split(key, 8)
        w = lambda k, sh: jax.random.normal(k, sh, jnp.float32) * 0.02
        return {'x': jax.random.normal(ks[0], (B, T, D_MODEL), jnp.float32), 'Wq_sem': w(ks[1], (D_MODEL, H * DS)), 'Wk_sem': w(ks[2], (D_MODEL, HKV * DS)), 'Wq_geo': w(ks[3], (D_MODEL, H * DG)), 'Wk_geo': w(ks[4], (D_MODEL, HKV * DG)), 'Wv': w(ks[5], (D_MODEL, HKV * DV)), 'Wo': w(ks[6], (H * DV, D_MODEL)), 'logit_scale': jnp.zeros((H,), jnp.float32)}
    _L0_attn_in = _L0_attn_setup()

    def _L0_ffn_setup():
        import jax, jax.numpy as jnp
        import numpy as np
        TOP_K = 4
        NUM_EXPERTS = 16
        key = jax.random.key(seed)
        ks = jax.random.split(key, 6)
        B, S, H, I, E = (2, 128, 256, 224, NUM_EXPERTS)
        return {'x': jax.random.normal(ks[0], (B, S, H), dtype=jnp.float32), 'router_w': jax.random.normal(ks[1], (E, H), dtype=jnp.float32) * 0.02, 'expert_bias': jnp.zeros((E,), dtype=jnp.float32), 'gate_proj': jax.random.normal(ks[2], (E, H, I), dtype=jnp.float32) * 0.02, 'up_proj': jax.random.normal(ks[3], (E, H, I), dtype=jnp.float32) * 0.02, 'down_proj': jax.random.normal(ks[4], (E, I, H), dtype=jnp.float32) * 0.02}
    _L0_ffn_in = _L0_ffn_setup()
    _d = {'L0_attn_x': _L0_attn_in['x'], 'L0_attn_Wq_sem': _L0_attn_in['Wq_sem'], 'L0_attn_Wk_sem': _L0_attn_in['Wk_sem'], 'L0_attn_Wq_geo': _L0_attn_in['Wq_geo'], 'L0_attn_Wk_geo': _L0_attn_in['Wk_geo'], 'L0_attn_Wv': _L0_attn_in['Wv'], 'L0_attn_Wo': _L0_attn_in['Wo'], 'L0_attn_logit_scale': _L0_attn_in['logit_scale'], 'L0_ffn_router_w': _L0_ffn_in['router_w'], 'L0_ffn_expert_bias': _L0_ffn_in['expert_bias'], 'L0_ffn_gate_proj': _L0_ffn_in['gate_proj'], 'L0_ffn_up_proj': _L0_ffn_in['up_proj'], 'L0_ffn_down_proj': _L0_ffn_in['down_proj']}
    _x0 = _d['L0_attn_x']
    _d['L0_attn_x'] = jax.random.normal(jax.random.fold_in(jax.random.key(seed), 1), (2, 1024, 256), dtype=_x0.dtype)
    del _x0
    return _d

def reference(L0_attn_x, L0_attn_Wq_sem, L0_attn_Wk_sem, L0_attn_Wq_geo, L0_attn_Wk_geo, L0_attn_Wv, L0_attn_Wo, L0_attn_logit_scale, L0_ffn_router_w, L0_ffn_expert_bias, L0_ffn_gate_proj, L0_ffn_up_proj, L0_ffn_down_proj):

    def _L0_attn_ref(x, Wq_sem, Wk_sem, Wq_geo, Wk_geo, Wv, Wo, logit_scale):
        import jax, jax.numpy as jnp
        import numpy as np
        D_MODEL = 256
        H = 16
        HKV = 4
        DS = 32
        DG = 32
        DV = 64
        B, T = (2, 512)
        MB = 64
        LW = 128
        ROPE_BASE = 10000.0
        NEG_INF = -1000000000.0

        def _rope(x, pos, base):
            d = x.shape[-1]
            inv_freq = 1.0 / base ** (jnp.arange(0, d, 2, dtype=jnp.float32) / d)
            ang = pos.astype(jnp.float32)[:, None] * inv_freq
            cos, sin = (jnp.cos(ang), jnp.sin(ang))
            x1, x2 = jnp.split(x, 2, axis=-1)
            return jnp.concatenate([x1 * cos - x2 * sin, x2 * cos + x1 * sin], axis=-1)
        Bq, Tq = (x.shape[0], x.shape[1])
        split = lambda y, h, d: y.reshape(Bq, Tq, h, d).transpose(0, 2, 1, 3)
        q_sem = split(x @ Wq_sem, H, DS)
        k_sem = split(x @ Wk_sem, HKV, DS)
        q_geo = split(x @ Wq_geo, H, DG)
        k_geo = split(x @ Wk_geo, HKV, DG)
        v = split(x @ Wv, HKV, DV)
        pos = jnp.arange(Tq)
        q_geo = _rope(q_geo, pos, ROPE_BASE)
        k_geo = _rope(k_geo, pos, ROPE_BASE)
        remote = Tq - LW
        nblk = remote // MB
        pool = lambda a: jnp.concatenate([a[:, :, :remote].reshape(Bq, HKV, nblk, MB, a.shape[-1]).mean(axis=3), a[:, :, remote:]], axis=2)
        k_sem2, k_geo2, v2 = (pool(k_sem), pool(k_geo), pool(v))
        k_pos = jnp.concatenate([jnp.arange(nblk) * MB + (MB - 1), jnp.arange(remote, Tq)])
        rep = lambda a: jnp.repeat(a, H // HKV, axis=1)
        k_sem2, k_geo2, v2 = (rep(k_sem2), rep(k_geo2), rep(v2))
        scores = jnp.einsum('bhqd,bhkd->bhqk', q_sem, k_sem2) * (1.0 / jnp.sqrt(float(DS))) + jnp.einsum('bhqd,bhkd->bhqk', q_geo, k_geo2) * (1.0 / jnp.sqrt(float(DG)))
        scores = scores * jnp.exp(logit_scale)[None, :, None, None]
        mask = k_pos[None, :] <= pos[:, None]
        scores = jnp.where(mask[None, None], scores, NEG_INF)
        probs = jax.nn.softmax(scores, axis=-1)
        out = jnp.einsum('bhqk,bhkd->bhqd', probs, v2)
        out = out.transpose(0, 2, 1, 3).reshape(Bq, Tq, H * DV)
        return out @ Wo

    def _L0_ffn_ref(x, router_w, expert_bias, gate_proj, up_proj, down_proj):
        import jax, jax.numpy as jnp
        import numpy as np
        TOP_K = 4
        NUM_EXPERTS = 16
        logits = jnp.einsum('bsh,eh->bse', x, router_w) + expert_bias
        scores = jax.nn.softmax(logits, axis=-1)
        top_w, top_idx = jax.lax.top_k(scores, TOP_K)
        top_w = top_w / jnp.sum(top_w, axis=-1, keepdims=True)
        g = jnp.einsum('bsh,khe->bske', x, gate_proj)
        u = jnp.einsum('bsh,khe->bske', x, up_proj)
        act = jax.nn.silu(g) * u
        out = jnp.einsum('bske,keh->bskh', act, down_proj)
        sel = jnp.take_along_axis(out, top_idx[..., None], axis=2)
        return jnp.sum(sel * top_w[..., None], axis=2)
    x = L0_attn_x
    xn = _layernorm(x, axis=-1)
    x = x + _L0_attn_ref(xn, L0_attn_Wq_sem, L0_attn_Wk_sem, L0_attn_Wq_geo, L0_attn_Wk_geo, L0_attn_Wv, L0_attn_Wo, L0_attn_logit_scale) + _L0_ffn_ref(xn, L0_ffn_router_w, L0_ffn_expert_bias, L0_ffn_gate_proj, L0_ffn_up_proj, L0_ffn_down_proj)
    return x

_drawn_inputs = setup_inputs


def setup_inputs(seed=0):
    import zlib

    import numpy as np

    out = dict(_drawn_inputs(seed))
    spreads = {'L0_attn_logit_scale': (0.0, 0.8), 'L0_ffn_expert_bias': (0.0, 0.8)}
    factors = {'L0_attn_Wq_sem': 8.0,
     'L0_attn_Wk_sem': 8.0,
     'L0_attn_Wq_geo': 8.0,
     'L0_attn_Wk_geo': 8.0,
     'L0_attn_Wv': 4.061,
     'L0_attn_Wo': 4.108,
     'L0_ffn_router_w': 8.0,
     'L0_ffn_gate_proj': 7.07,
     'L0_ffn_up_proj': 6.986,
     'L0_ffn_down_proj': 6.98}
    for name, (base, spread) in spreads.items():
        noise = np.random.default_rng([zlib.crc32(name.encode()), seed]).standard_normal(out[name].shape)
        drawn = base * np.exp(spread * noise) if base else spread * noise
        out[name] = jnp.asarray(drawn.astype(out[name].dtype))
    for name, factor in factors.items():
        out[name] = (out[name] * factor).astype(out[name].dtype)
    return out
```

```python
from contextlib import ExitStack

import concourse.bass as bass
from concourse import mybir

F32 = mybir.dt.float32
F32R = mybir.dt.float32r
I32 = mybir.dt.int32
U32 = mybir.dt.uint32
ALU = mybir.AluOpType
ACT = mybir.ActivationFunctionType
AX = mybir.AxisListType

P = 128
NB, T, D = 2, 1024, 256
N = NB * T
TB = T // P
NT = N // P
DC = D // P
H, HKV, DS, DV = 16, 4, 32, 64
G = H // HKV
MB, LW = 64, 128
NBLK = (T - LW) // MB
NKEY = NBLK + LW
HK = H * NBLK
HALF = HK // 2
E, K, I = 16, 4, 224
IH = I // 2
NS = N * K // P + E - 1
NROW = N * K
EPS = 1e-5
NEG = -1e9
SCALE = 1.0 / float(DS) ** 0.5
DMA = 16

CA = {}
_at = 0
for _name, _n in (("ident", P), ("below", P), ("pool", 2), ("cos", TB * 32), ("sin", TB * 32), ("iota_e", E),
                  ("iota_j", NS), ("iota_p", P), ("dest", NT * K), ("trash", NS), ("pad_row", 1), ("carry", E * NT)):
    CA[_name] = (_at, _n)
    _at += _n
NCA = _at
CC = {}
_at = 0
for _name, _n in (("heads", H), ("pair", 2), ("see", TB * NBLK), ("hide", TB * NBLK), ("more", TB), ("even", TB),
                  ("see_l", NKEY), ("hide_l", NKEY), ("copies", HKV * P)):
    CC[_name] = (_at, _n)
    _at += _n
NCC = _at


def build(nc, x, wq_sem, wk_sem, wq_geo, wk_geo, wv, wo, logit_scale, router_w, expert_bias, gate, up, down,
          const_a, const_c, out):
    x_rows = x.rearrange("b t d -> (b t) d")
    out_rows = out.rearrange("b t d -> (b t) d")
    xn_d = nc.dram_tensor("xn_rows", (N + P, D), F32, kind="Internal").ap()
    y_d = nc.dram_tensor("expert_rows", (NROW + NS * P, D), F32, kind="Internal").ap()
    ds = bass.ds

    ctx = ExitStack()
    with ctx:
        base = (nc.sbuf_base + 63) // 64 * 64
        names = [0]

        class Region:
            def __init__(self, start, size):
                self.start, self.at, self.end = start, start, start + size

            def take(self, name, shape, dtype=F32):
                size = 4
                for n in shape[1:]:
                    size *= n
                size = (size + 31) // 32 * 32
                assert self.at + size <= self.end, (name, self.at + size - self.end)
                t = nc.alloc_sbuf_tensor_at(name, list(shape), dtype, offset=self.at)
                self.at += size
                return t

        WGU, WDN = DC * 2 * I, 2 * D
        BIG = E * (WGU + WDN) * 2 * 4
        WORK, STAGE, KEEP = 16384, 2 * (WGU + WDN) * 4, 10816
        ctx.enter_context(nc.sbuf_tensor("arena", [P, (BIG + WORK + STAGE + KEEP + 128) // 4], F32))
        r_big, r_late = Region(base, BIG), Region(base, BIG)
        r_work = [Region(base + BIG, WORK) for _ in range(3)]
        r_stage = [Region(base + BIG + WORK, STAGE) for _ in range(2)]
        r_keep = Region(base + BIG + WORK + STAGE, KEEP)

        wgu_h = r_big.take("wgu_hi", [P, E * WGU], F32R)
        wdn_h = r_big.take("wdn_hi", [IH, E * WDN], F32R)
        wgu_l = r_big.take("wgu_lo", [P, E * WGU], F32R)
        wdn_l = r_big.take("wdn_lo", [IH, E * WDN], F32R)
        LATE = E // 2
        r_x = Region(r_big.at - (E - LATE) * WDN * 4, NB * TB * D * 4)
        x_all = r_x.take("x_all", [P, TB, NB, D])
        stage = [r_stage[0].take(f"stage{s}", [P, WGU + WDN]) for s in range(2)]

        ca = r_keep.take("const_a", [P, NCA])
        x_keys = r_keep.take("x_keys", [P, DC, NB, NKEY])
        kgeo_t = r_keep.take("kgeo_t", [P, NB, NKEY])
        weight = r_keep.take("choice_weight", [P, NT, K])
        dest_i = r_keep.take("dest_i", [P, NS], I32)
        tok_i = r_keep.take("tok_i", [P, NS], I32)
        te_i = r_keep.take("tile_expert", [1, NS], I32)
        idx_in = [r_keep.take(f"idx_in{p}", [P, 1], I32) for p in range(2)]
        idx_out = [r_keep.take(f"idx_out{p}", [P, 1], I32) for p in range(2)]

        wa = r_work[0]
        xnb = [wa.take(f"xn{u}", [P, D]) for u in range(2)]
        xT = [wa.take(f"xT{u}", [P, DC, P]) for u in range(2)]
        krot = [wa.take(f"krot{u}", [P, HKV * DS]) for u in range(2)]
        rope1 = [wa.take(f"rope1_{u}", [P, HKV * DS]) for u in range(2)]
        rope2 = [wa.take(f"rope2_{u}", [P, HKV * DS]) for u in range(2)]
        wkg = wa.take("wkg", [P, DC, HKV * DS])
        rw = wa.take("router_rows", [E, D])
        rwT = wa.take("router_t", [P, DC, E])
        ebias = wa.take("ebias", [P, E])
        stats = wa.take("stats", [P, NT, 6])
        mean, var, dif, rstd, tmp = (wa.take(n, [P, NT]) for n in ("mean", "var", "dif", "rstd", "tmp"))
        zero = wa.take("zero", [P, D])
        wr = r_work[1]
        logit = wr.take("logit", [P, NT, E])
        assert wr.at <= wa.end
        top = wr.take("top", [P, NT, 8])
        topi = wr.take("topi", [P, NT, 8], U32)
        topf = wr.take("topf", [P, NT, K])
        wt = Region(wr.at, 5376)
        hot = wr.take("hot", [P, NT, K, E])
        sel = wr.take("sel", [P, NT, E])
        tot = wr.take("tot", [P, E, NT])
        cum = wr.take("cum", [P, E, NT])
        cnt, nt_f, ends = (wr.take(n, [P, E]) for n in ("cnt", "nt_f", "ends"))
        nt_i = wr.take("nt_i", [P, E], I32)
        wsum = wr.take("wsum", [P, NT])
        pos = wr.take("pos", [P, NT * K])
        pos_i = wr.take("pos_i", [P, NT * K], I32)
        jf = wr.take("pos_tile", [P, NT * K])
        rf = wr.take("pos_row", [P, NT * K])
        onehot_p = [wr.take(f"onehot_p{q}", [P, P]) for q in range(2)]
        onehot_j = [wr.take(f"onehot_j{q}", [P, NS]) for q in range(2)]
        ones = wr.take("ones", [P, P])
        cmp_j = wt.take("cmp_j", [1, NS, E])
        te_f = wt.take("te_f", [1, NS])
        wt = Region(wt.start, 5376)
        dest_f = wt.take("dest_f", [P, NS])
        pad_f = wt.take("pad_f", [P, NS])
        tok_lo = wt.take("tok_lo", [P, NS], I32)
        tok_hi = wt.take("tok_hi", [P, NS], I32)
        assert wt.at <= wr.at
        wb = r_work[2]
        xg = [wb.take(f"xg{p}", [P, D]) for p in range(2)]
        xh = [wb.take(f"xh{p}", [P, DC, P], F32R) for p in range(2)]
        xl = [wb.take(f"xl{p}", [P, DC, P], F32R) for p in range(2)]
        sg = [wb.take(f"sg{p}", [P, I]) for p in range(2)]
        av = [wb.take(f"act{p}", [P, I]) for p in range(2)]
        ah = [wb.take(f"ah{p}", [IH, 2, P], F32R) for p in range(2)]
        al = [wb.take(f"al{p}", [IH, 2, P], F32R) for p in range(2)]
        ysb = [wb.take(f"y{p}", [P, D]) for p in range(2)]
        ws = r_stage[1]
        wqg = ws.take("wqg", [P, DC, H * DS])
        wqs = ws.take("wqs", [P, DC, H * DS])
        wv_s = ws.take("wv_s", [P, DC, HKV * DV])
        wks = ws.take("wks", [P, DC, HKV * DS])
        wc = r_late
        cc = wc.take("const_c", [P, NCC])
        wo_s = wc.take("wo_s", [P, H // 2, D])
        lscale = wc.take("lscale", [P, H])
        hmask = wc.take("hmask", [P, H])
        wk_rep = wc.take("wk_rep", [P, DC, HKV, G, DS])
        wv_rep = wc.take("wv_rep", [P, DC, HKV, 2, DV])
        wqT = wc.take("wqT", [P, HKV, D])
        bd_s = wc.take("bd_s", [P, NB, HKV, G, NKEY])
        bd_g = wc.take("bd_g", [P, NB, HKV, G, NKEY])
        asem = wc.take("asem", [P, NB, DC, HK])
        vb = wc.take("vb", [P, NB, 12, HALF + 1])
        vw = wc.take("vw", [HALF + 1, NB, 2, D])
        vloc = wc.take("vloc", [P, NB, HKV * DV])
        xc = [wc.take(f"xc{u}", [P, D]) for u in range(2)]
        xr = [wc.take(f"xr{u}", [P, D]) for u in range(2)]
        yv = [wc.take(f"yv{u}", [P, K, D]) for u in range(2)]
        xcT = [wc.take(f"xcT{u}", [P, DC, P]) for u in range(2)]
        q1 = [wc.take(f"q1_{u}", [P, H, DS]) for u in range(2)]
        q2 = [wc.take(f"q2_{u}", [P, H, DS]) for u in range(2)]
        qr = [wc.take(f"qr{u}", [P, H * DS]) for u in range(2)]
        qrT = [wc.take(f"qrT{u}", [P, HKV, P]) for u in range(2)]
        s1 = [wc.take(f"s1_{u}", [P, H, NBLK]) for u in range(2)]
        s2 = [wc.take(f"s2_{u}", [P, H, NBLK]) for u in range(2)]
        sd = [wc.take(f"sd{u}", [P, H, NBLK]) for u in range(2)]
        ex = [wc.take(f"ex{u}", [P, H, NBLK]) for u in range(2)]
        smax, ssum, sfull, srec = ([wc.take(f"{n}{u}", [P, H]) for u in range(2)] for n in ("smax", "ssum", "sfull", "srec"))
        pr = [wc.take(f"pr{u}", [P, HK + 1]) for u in range(2)]
        prT = [wc.take(f"prT{u}", [HALF + 1, 2, P]) for u in range(2)]
        acc = [[wc.take(f"acc{u}_{k}", [P, D]) for k in range(5)] for u in range(2)]
        qs = wc.take("qs", [P, H * DS])
        qsT = wc.take("qsT", [P, HKV, P])
        l1 = wc.take("l1", [P, G, NKEY])
        l2 = wc.take("l2", [P, G, NKEY])
        l3 = wc.take("l3", [P, G, NKEY])
        lex = wc.take("lex", [P, G, NKEY])
        lmax, lsum, lrec = (wc.take(n, [P, G]) for n in ("lmax", "lsum", "lrec"))
        lp = [wc.take(f"lp{q}", [P, G, LW]) for q in range(2)]
        lpT = [wc.take(f"lpT{q}", [P, G, P]) for q in range(2)]
        osb = wc.take("osb", [P, H * DV])
        oT = wc.take("oT", [P, H // 2, P])

        bank = [ctx.enter_context(nc.psum_tensor(f"bank{n}", [P, 512], F32)) for n in range(8)]

        def const(t, table, name):
            at, n = table[name]
            return t[:, at:at + n]

        ident = const(ca, CA, "ident")
        below = const(ca, CA, "below")
        pool2 = const(ca, CA, "pool")

        def sem(name):
            return ctx.enter_context(nc.semaphore(name))

        def pair(name):
            return [sem(f"{name}{p}") for p in range(2)]

        const_in, bias_in, zero_ready, zero_stored = sem("const_in"), sem("bias_in"), sem("zero_ready"), sem("zero_stored")
        x_in = [sem(f"x_in{q}") for q in range(4)]
        dve_step, rw_t, rwT_ready, var_ready, std_ready = sem("dve_step"), sem("rw_t"), sem("rwT_ready"), sem("var_ready"), sem("std_ready")
        w_in, w_hi, w_lo = pair("w_in"), pair("w_hi"), pair("w_lo")
        xn_ready, xn_turned, xT_ready = pair("xn_ready"), pair("xn_turned"), pair("xT_ready")
        k_raw, rope_half, krot_ready, pooled, xn_stored = pair("k_raw"), pair("rope_half"), pair("krot_ready"), pair("pooled"), pair("xn_stored")
        keys_turned, keys_kept = pair("keys_turned"), sem("keys_kept")
        soft_in, soft_out, sel_ready, ranked = sem("soft_in"), sem("soft_out"), sem("sel_ready"), sem("ranked")
        pair_ready, pair_used, inverse_done = pair("pair_ready"), pair("pair_used"), sem("inverse_done")
        lists_ready = sem("lists_ready")
        in_idx, out_idx, gathered, x_turned, xh_ready, xl_ready = (pair(n) for n in ("in_idx", "out_idx", "gathered", "x_turned", "xh_ready", "xl_ready"))
        gu_done, sg_ready, av_ready, av_turned, ah_ready, al_ready = (pair(n) for n in ("gu_done", "sg_ready", "av_ready", "av_turned", "ah_ready", "al_ready"))
        y_done, y_ready, scattered = pair("y_done"), pair("y_ready"), pair("scattered")
        wc_in, wo_in = sem("wc_in"), sem("wo_in")
        rep_ready, c_step, set_pe, set_act, set_dve = sem("rep_ready"), sem("c_step"), sem("set_pe"), sem("set_act"), sem("set_dve")
        xc_in, xr_in, yv_in = pair("xc_in"), pair("xr_in"), pair("yv_in")
        c_xt, c_xT, c_q, c_roped, c_qr, c_qt, c_qT, c_s, c_d, c_ex, c_p, c_pt, c_pT, c_o, c_out, c_stored = (
            pair("c_" + n) for n in ("x_turned", "xT_ready", "q_done", "roped", "q_ready", "q_turned", "qT_ready", "s_done",
                                     "d_ready", "exp_ready", "p_ready", "p_turned", "pT_ready", "o_done", "out_ready", "out_stored"))
        c_link, c_sum = pair("c_link"), pair("c_sum")
        l_pe, l_act, l_dve = sem("l_pe"), sem("l_act"), sem("l_dve")

        block = ctx.enter_context(nc.Block())

        def tile_rows(dram, t):
            return dram[ds(t * P, P), :]

        TILES = [(NS + 1) // 2, NS // 2]
        LOOP = (NS - 3) // 2
        assert 2 * LOOP + 3 == NS
        REMOTE = TB - 1

        def of(j, d):
            p, n = j
            return (p + d) % 2, n + (p + d) // 2

        def steps(eng, step):
            for j in (-2, -1, 0):
                step((j % 2, j // 2), j)
            with eng.Fori(0, LOOP) as i:
                step((1, i), None)
                step((0, i + 1), None)
            for j in (NS - 2, NS - 1, NS):
                step((j % 2, j // 2), j)

        def has(j, d):
            return j is None or 0 <= j + d < NS

        @block.sync
        def _(sp):
            sp.dma_start(ca[:, :], const_a).then_inc(const_in, DMA)
            x_v = x.rearrange("b (t p) d -> p b t d", p=P)
            for q in range(4):
                for b in range(NB):
                    sp.dma_start(x_all[:, 2 * q:2 * q + 2, b, :], x_v[:, b, 2 * q:2 * q + 2, :]).then_inc(x_in[q], DMA)
            sp.dma_start(rw[:, :], router_w).then_inc(const_in, DMA)
            sp.dma_start(wkg[:, :, :], wk_geo.rearrange("(c p) n -> p c n", p=P)).then_inc(const_in, DMA)
            sp.dma_start(ebias[:, :], expert_bias.rearrange("(a e) -> a e", a=1).to_broadcast([P, E])).then_inc(bias_in, DMA)
            sp.wait_ge(zero_ready, 1)
            sp.dma_start(xn_d[N:N + P, :], zero[:, :]).then_inc(zero_stored, DMA)

            gate_v = gate.rearrange("e (c p) n -> p e c n", p=P)
            up_v = up.rearrange("e (c p) n -> p e c n", p=P)
            down_v = down.rearrange("e (c p) n -> p e c n", p=IH)

            def load_expert(i, s):
                e = 2 * i + s
                sp.wait_ge(w_lo[s], i)
                gu = stage[s][:, 0:WGU].rearrange("p (c n) -> p c n", c=DC)
                dn = stage[s][0:IH, WGU:WGU + WDN].rearrange("p (c n) -> p c n", c=2)
                sp.dma_start(gu[:, :, 0:I], gate_v[:, ds(e, 1), :, :].rearrange("p o c n -> p (o c) n")).then_inc(w_in[s], DMA)
                sp.dma_start(gu[:, :, I:2 * I], up_v[:, ds(e, 1), :, :].rearrange("p o c n -> p (o c) n")).then_inc(w_in[s], DMA)
                sp.dma_start(dn, down_v[:, ds(e, 1), :, :].rearrange("p o c n -> p (o c) n")).then_inc(w_in[s], DMA)

            with sp.Fori(0, E // 2) as i:
                load_expert(i, 0)
                load_expert(i, 1)
            sp.wait_ge(w_lo[0], E // 2)
            sp.wait_ge(w_lo[1], E // 2)
            for t, w in ((wqg, wq_geo), (wqs, wq_sem), (wv_s, wv), (wks, wk_sem)):
                sp.dma_start(t[:, :, :], w.rearrange("(c p) n -> p c n", p=P)).then_inc(wc_in, DMA)
            for p in range(2):
                sp.wait_ge(y_done[p], TILES[p])
            sp.dma_start(cc[:, :], const_c).then_inc(wo_in, DMA)
            sp.dma_start(lscale[:, :], logit_scale.rearrange("(a h) -> a h", a=1).to_broadcast([P, H])).then_inc(wo_in, DMA)
            sp.dma_start(wo_s[:, :, :], wo.rearrange("(c p) n -> p c n", p=P)).then_inc(wo_in, DMA)
            y_v = y_d.rearrange("(t p) n -> p t n", p=P)

            def load_tile(i, u):
                t = u * TB + i
                sp.wait_ge(c_xt[u], i)
                sp.dma_start(xc[u][:, :], tile_rows(xn_d, t)).then_inc(xc_in[u], DMA)
                sp.wait_ge(c_out[u], i)
                sp.dma_start(xr[u][:, :], tile_rows(x_rows, t)).then_inc(xr_in[u], DMA)
                sp.dma_start(yv[u][:, :, :], y_v[:, ds(t * K, K), :]).then_inc(yv_in[u], DMA)

            for p in range(2):
                sp.wait_ge(xn_stored[p], TB * DMA)
                sp.wait_ge(scattered[p], TILES[p] * DMA)
            with sp.Fori(0, REMOTE) as i:
                load_tile(i, 0)
                load_tile(i, 1)
            for u in range(NB):
                load_tile(REMOTE, u)
            for u in range(NB):
                sp.wait_ge(c_stored[u], TB * DMA)

        @block.gpsimd
        def _(gp):
            nc.gpsimd.memset(zero[:, :], 0.0).then_inc(zero_ready, 1)

            def split_low(i, s):
                e = 2 * i + s
                gp.wait_ge(w_hi[s], i + 1)
                gu, dn = ds(e * WGU, WGU), ds(e * WDN, WDN)
                nc.gpsimd.tensor_tensor(wgu_l[:, gu], stage[s][:, 0:WGU], wgu_h[:, gu].bitcast(F32), ALU.subtract)
                nc.gpsimd.tensor_tensor(wdn_l[:, dn], stage[s][0:IH, WGU:WGU + WDN], wdn_h[:, dn].bitcast(F32),
                                        ALU.subtract).then_inc(w_lo[s], 1)

            with gp.Fori(0, LATE // 2) as i:
                split_low(i, 0)
                split_low(i, 1)
            with gp.Fori(LATE // 2, E // 2) as i:
                for s in range(2):
                    for u in range(NB):
                        gp.wait_ge(xn_ready[u], 2 * i + (s + 1 - LATE))
                    split_low(i, s)

            for p in range(2):
                gp.wait_ge(xn_stored[p], TB * DMA)
            gp.wait_ge(zero_stored, DMA)

            def gather(p, n, n_next):
                gp.wait_ge(zero_stored, DMA)
                gp.wait_ge(in_idx[p], n_next)
                gp.wait_ge(x_turned[p], n)
                gp.indirect_dma_start(xg[p][:, :], None, xn_d, bass.IndirectOffsetOnAxis(idx_in[p][:, 0:1], 0)).then_inc(gathered[p], DMA)

            def scatter(p, n_next):
                gp.wait_ge(lists_ready, 1)
                gp.wait_ge(out_idx[p], n_next)
                gp.wait_ge(y_ready[p], n_next)
                gp.indirect_dma_start(y_d, bass.IndirectOffsetOnAxis(idx_out[p][:, 0:1], 0), ysb[p][:, :], None).then_inc(scattered[p], DMA)

            AHEAD = 6
            for j in range(AHEAD):
                gather(j % 2, j // 2, j // 2 + 1)
            FULL = (NS - AHEAD) // 2
            with gp.Fori(0, FULL) as i:
                g_now, g_next, s_next = (gp.to_reg(i + n) for n in (AHEAD // 2, AHEAD // 2 + 1, 1))
                for p in range(2):
                    gather(p, g_now, g_next)
                    scatter(p, s_next)
            for j in range(2 * FULL, NS):
                if j + AHEAD < NS:
                    gather(j % 2, j // 2 + AHEAD // 2, j // 2 + AHEAD // 2 + 1)
                scatter(j % 2, j // 2 + 1)

            def rope_sum(i, u):
                gp.wait_ge(c_roped[u], i + 1)
                gp.wait_ge(c_qt[u], i)
                nc.gpsimd.tensor_tensor(qr[u][:, :], q1[u][:, :, :].rearrange("p h d -> p (h d)"),
                                        q2[u][:, :, :].rearrange("p h d -> p (h d)"), ALU.add).then_inc(c_qr[u], 1)

            with gp.Fori(0, REMOTE) as i:
                rope_sum(i, 0)
                rope_sum(i, 1)
            for u in range(NB):
                rope_sum(REMOTE, u)

        @block.scalar
        def _(act):
            act.wait_ge(var_ready, 1)
            nc.scalar.activation(tmp[:, :], var[:, :], ACT.Sqrt).then_inc(std_ready, 1)

            def ln_tile(i, u):
                act.wait_ge(xn_ready[u], i + 1)
                act.dma_start(tile_rows(xn_d, u * TB + i), xnb[u][:, :]).then_inc(xn_stored[u], DMA)
                act.wait_ge(xn_turned[u], i + 1)
                act.wait_ge(k_raw[u], i)
                nc.scalar.copy(xT[u][:, :, :], bank[u][:, 0:D].rearrange("p (c n) -> p c n", c=DC)).then_inc(xT_ready[u], 1)

            def split_high(i, s):
                e = 2 * i + s
                act.wait_ge(w_in[s], (i + 1) * 3 * DMA)
                nc.scalar.copy(wgu_h[:, ds(e * WGU, WGU)], stage[s][:, 0:WGU])
                nc.scalar.copy(wdn_h[:, ds(e * WDN, WDN)], stage[s][0:IH, WGU:WGU + WDN]).then_inc(w_hi[s], 1)

            with act.Fori(0, REMOTE) as i:
                ln_tile(i, 0)
                ln_tile(i, 1)
                split_high(i, 0)
                split_high(i, 1)
            for u in range(NB):
                ln_tile(REMOTE, u)
            for u in range(NB):
                split_high(REMOTE, u)

            for u in range(NB):
                act.wait_ge(keys_turned[u], 1)
                pb = bank[5 + u]
                nc.scalar.copy(kgeo_t[:, u, 0:NBLK], pb[:, 0:NBLK])
                nc.scalar.copy(kgeo_t[:, u, NBLK:NKEY], pb[:, 64:64 + LW])
                nc.scalar.copy(x_keys[:, :, u, 0:NBLK], pb[:, NBLK:NBLK * 3].rearrange("p (c n) -> p c n", c=DC))
                nc.scalar.copy(x_keys[:, :, u, NBLK:NKEY], xT[u][:, :, :]).then_inc(keys_kept, 1)

            act.wait_ge(soft_in, 1)
            nc.scalar.activation(weight[:, :, :], weight[:, :, :], ACT.Exp).then_inc(soft_out, 1)

            def step(j, at):
                if has(at, 2):
                    p, n = of(j, 2)
                    act.wait_ge(x_turned[p], n + 1)
                    if at is None or at > 0:
                        act.wait_ge(gu_done[p], n)
                    nc.scalar.copy(xh[p][:, :, :], bank[p][:, 0:D].rearrange("p (c n) -> p c n", c=DC)).then_inc(xh_ready[p], 1)
                if has(at, 1):
                    p, n = of(j, 1)
                    act.wait_ge(gu_done[p], n + 1)
                    act.wait_ge(av_ready[p], n)
                    nc.scalar.activation(sg[p][:, :], bank[2 + p][:, 0:I], ACT.Silu).then_inc(sg_ready[p], 1)
                if has(at, 0):
                    p, n = j
                    act.wait_ge(av_turned[p], n + 1)
                    act.wait_ge(y_done[p], n)
                    nc.scalar.copy(ah[p][:, :, :], bank[4 + p][0:IH, 0:2 * P].rearrange("p (c n) -> p c n", c=2)).then_inc(ah_ready[p], 1)
                if has(at, -1):
                    p, n = of(j, -1)
                    act.wait_ge(y_done[p], n + 1)
                    act.wait_ge(scattered[p], n * DMA)
                    nc.scalar.copy(ysb[p][:, :], bank[6 + p][:, 0:D]).then_inc(y_ready[p], 1)

            steps(act, step)

            act.wait_ge(wc_in, 4 * DMA)
            act.wait_ge(wo_in, 3 * DMA)
            for c in range(DC):
                for n in range(G):
                    nc.scalar.copy(wk_rep[:, c, :, n, :], wks[:, c, :].rearrange("p (g d) -> p g d", g=HKV))
                for n in range(2):
                    nc.scalar.copy(wv_rep[:, c, :, n, :], wv_s[:, c, :].rearrange("p (g d) -> p g d", g=HKV))
            nc.scalar.activation(lscale[:, :], lscale[:, :], ACT.Exp).then_inc(rep_ready, 1)
            act.wait_ge(set_pe, 1)
            for g in range(HKV):
                last = nc.scalar.copy(wqT[:, g, :], bank[g][:, 0:D])
            last.then_inc(set_act, 1)
            for b in range(NB):
                act.wait_ge(set_pe, 3 + 4 * b)
                nc.scalar.copy(asem[:, b, :, :], bank[0][:, 0:DC * HK].rearrange("p (c n) -> p c n", c=DC)).then_inc(set_act, 1)
                act.wait_ge(set_pe, 5 + 4 * b)
                nc.scalar.copy(vw[0:HALF, b, 0, :], bank[1][0:HALF, 0:D])
                nc.scalar.copy(vw[:, b, 1, :], bank[2][0:HALF + 1, 0:D])
                nc.scalar.copy(vloc[:, b, :], bank[3][:, 0:HKV * DV]).then_inc(set_act, 1)

            def x_keep(i, u):
                act.wait_ge(c_xt[u], i + 1)
                act.wait_ge(c_s[u], i)
                nc.scalar.copy(xcT[u][:, :, :], bank[u][:, 0:D].rearrange("p (c n) -> p c n", c=DC)).then_inc(c_xT[u], 1)

            def q_keep(i, u):
                act.wait_ge(c_qt[u], i + 1)
                nc.scalar.copy(qrT[u][:, :, :], bank[4 + u][:, :].rearrange("p (g n) -> p g n", g=HKV)).then_inc(c_qT[u], 1)

            def p_keep(i, u):
                act.wait_ge(c_pt[u], i + 1)
                nc.scalar.copy(prT[u][0:HALF, 0, :], bank[u][0:HALF, 0:P])
                nc.scalar.copy(prT[u][:, 1, :], bank[u][0:HALF + 1, P:2 * P]).then_inc(c_pT[u], 1)

            def store(i, u):
                act.wait_ge(c_out[u], i + 1)
                act.dma_start(tile_rows(out_rows, u * TB + i), acc[u][4][:, :]).then_inc(c_stored[u], DMA)

            with act.Fori(0, REMOTE) as i:
                for u in range(NB):
                    x_keep(i, u)
                for u in range(NB):
                    q_keep(i, u)
                for u in range(NB):
                    act.wait_ge(c_d[u], i + 1)
                    nc.scalar.activation(ex[u][:, :, :], sd[u][:, :, :], ACT.Exp).then_inc(c_ex[u], 1)
                for u in range(NB):
                    p_keep(i, u)
                for u in range(NB):
                    store(i, u)

            n_pe = 0
            for u in range(NB):
                x_keep(REMOTE, u)
                n_pe += 1
                act.wait_ge(l_pe, n_pe)
                nc.scalar.copy(qs[:, :], bank[6][:, :]).then_inc(l_act, 1)
                q_keep(REMOTE, u)
                n_pe += 1
                act.wait_ge(l_pe, n_pe)
                nc.scalar.copy(qsT[:, :, :], bank[5 - u][:, :].rearrange("p (g n) -> p g n", g=HKV)).then_inc(l_act, 1)
                for g in range(HKV):
                    act.wait_ge(l_dve, (u * HKV + g) * 3 + 2)
                    nc.scalar.activation(lex[:, :, :], l3[:, :, :], ACT.Exp).then_inc(l_act, 1)
                    n_pe += 2
                    act.wait_ge(l_pe, n_pe)
                    nc.scalar.copy(lpT[g % 2][:, :, :], bank[7][:, :].rearrange("p (h n) -> p h n", h=G)).then_inc(l_act, 1)
                    n_pe += 1
                    act.wait_ge(l_pe, n_pe)
                    nc.scalar.copy(osb[:, g * G * DV:(g + 1) * G * DV], bank[6][:, 0:G * DV]).then_inc(l_act, 1)
                n_pe += 1
                act.wait_ge(l_pe, n_pe)
                nc.scalar.copy(oT[:, 0:4, :], bank[4][:, :].rearrange("p (h n) -> p h n", h=4))
                nc.scalar.copy(oT[:, 4:8, :], bank[5][:, :].rearrange("p (h n) -> p h n", h=4)).then_inc(l_act, 1)
                p_keep(REMOTE, u)
                store(REMOTE, u)

        @block.vector
        def _(dve):
            count = [0]

            def link(ins):
                count[0] += 1
                ins.then_inc(dve_step, 1)
                dve.wait_ge(dve_step, count[0])

            dve.wait_ge(rw_t, 1)
            nc.vector.tensor_copy(rwT[:, :, :], bank[7][:, 0:DC * E].rearrange("p (c n) -> p c n", c=DC)).then_inc(rwT_ready, 1)

            for q in range(4):
                dve.wait_ge(x_in[q], NB * DMA)
                for b in range(NB):
                    for t in range(2 * q, 2 * q + 2):
                        last = nc.vector.bn_stats(stats[:, b * TB + t, :], x_all[:, t, b, :])
            link(last)
            link(nc.vector.tensor_tensor(mean[:, :], stats[:, :, 1], stats[:, :, 4], ALU.add))
            link(nc.vector.tensor_tensor(dif[:, :], stats[:, :, 1], stats[:, :, 4], ALU.subtract))
            link(nc.vector.tensor_tensor(var[:, :], stats[:, :, 2], stats[:, :, 5], ALU.add))
            link(nc.vector.tensor_scalar(mean[:, :], mean[:, :], 0.5, None, ALU.mult))
            link(nc.vector.tensor_tensor(tmp[:, :], dif[:, :], dif[:, :], ALU.mult))
            link(nc.vector.tensor_scalar(var[:, :], var[:, :], 1.0 / D, EPS, ALU.mult, ALU.add))
            nc.vector.scalar_tensor_tensor(var[:, :], tmp[:, :], 0.25, var[:, :], ALU.mult, ALU.add).then_inc(var_ready, 1)
            dve.wait_ge(var_ready, 1)
            dve.wait_ge(std_ready, 1)
            link(nc.vector.reciprocal(rstd[:, :], tmp[:, :]))
            link(nc.vector.tensor_tensor(dif[:, :], rstd[:, :], rstd[:, :], ALU.mult))
            link(nc.vector.tensor_tensor(dif[:, :], dif[:, :], var[:, :], ALU.mult))
            link(nc.vector.tensor_scalar(dif[:, :], dif[:, :], -0.5, 1.5, ALU.mult, ALU.add))
            link(nc.vector.tensor_tensor(rstd[:, :], rstd[:, :], dif[:, :], ALU.mult))

            def normalise(i, u):
                t = u * TB + i
                dve.wait_ge(pooled[u], i)
                dve.wait_ge(xn_stored[u], i * DMA)
                xrow = x_all[:, :, :, :].rearrange("p t b d -> p (t b d)")[:, ds((i * NB + u) * D, D)]
                nc.vector.tensor_scalar(xnb[u][:, :], xrow, mean[:, ds(t, 1)], rstd[:, ds(t, 1)],
                                        ALU.subtract, ALU.mult).then_inc(xn_ready[u], 1)

            cos = const(ca, CA, "cos")
            sin = const(ca, CA, "sin")

            def rope_k(i, u):
                dve.wait_ge(k_raw[u], i + 1)
                raw = bank[3 + u][:, 0:HKV * DS].rearrange("p (g h d) -> p g h d", g=HKV, h=2)
                r1 = rope1[u][:, :].rearrange("p (g d) -> p g d", g=HKV)
                r2 = rope2[u][:, :].rearrange("p (g h d) -> p g h d", g=HKV, h=2)
                co = cos[:, ds(i * DS, DS)].rearrange("p (o d) -> p o d", o=1).to_broadcast([P, HKV, DS])
                s_lo = sin[:, ds(i * DS, DS // 2)].rearrange("p (o d) -> p o d", o=1).to_broadcast([P, HKV, DS // 2])
                s_hi = sin[:, ds(i * DS + DS // 2, DS // 2)].rearrange("p (o d) -> p o d", o=1).to_broadcast([P, HKV, DS // 2])
                nc.vector.tensor_tensor(r1, bank[3 + u][:, 0:HKV * DS].rearrange("p (g d) -> p g d", g=HKV), co, ALU.mult)
                nc.vector.tensor_tensor(r2[:, :, 0, :], raw[:, :, 1, :], s_lo, ALU.mult)
                nc.vector.tensor_tensor(r2[:, :, 1, :], raw[:, :, 0, :], s_hi, ALU.mult).then_inc(rope_half[u], 1)
                dve.wait_ge(rope_half[u], i + 1)
                nc.vector.tensor_tensor(krot[u][:, :], rope1[u][:, :], rope2[u][:, :], ALU.add).then_inc(krot_ready[u], 1)

            dve.wait_ge(const_in, 3 * DMA)
            with dve.Fori(0, REMOTE) as i:
                for u in range(NB):
                    normalise(i, u)
                for u in range(NB):
                    rope_k(i, u)
            for u in range(NB):
                normalise(REMOTE, u)
            for u in range(NB):
                rope_k(REMOTE, u)

            dve.wait_ge(bias_in, DMA)
            for u in range(NB):
                dve.wait_ge(k_raw[u], TB)
                dve.wait_ge(xn_stored[u], TB * DMA)
            dve.wait_ge(zero_stored, DMA)
            dve.wait_ge(keys_kept, NB)
            link(nc.vector.tensor_tensor(logit[:, :, :], bank[2][:, 0:NT * E].rearrange("p (t e) -> p t e", t=NT),
                                         ebias[:, :].rearrange("p (o e) -> p o e", o=1).to_broadcast([P, NT, E]), ALU.add))
            for t in range(NT):
                last = nc.vector.max(top[:, t, :], logit[:, t, :])
            link(last)
            nc.vector.tensor_tensor(weight[:, :, :], top[:, :, 0:K], top[:, :, 0:1].to_broadcast([P, NT, K]),
                                    ALU.subtract).then_inc(soft_in, 1)
            for t in range(NT):
                last = nc.vector.max_index(topi[:, t, :], top[:, t, :], logit[:, t, :])
            link(last)
            link(nc.vector.tensor_copy(topf[:, :, :], topi[:, :, 0:K]))
            iota_e = const(ca, CA, "iota_e")
            link(nc.vector.tensor_tensor(
                hot[:, :, :, :].rearrange("p t k e -> p (t k) e"),
                iota_e.rearrange("p (o e) -> p o e", o=1).to_broadcast([P, NT * K, E]),
                topf[:, :, :].rearrange("p t (k o) -> p (t k) o", o=1).to_broadcast([P, NT * K, E]), ALU.is_equal))
            link(nc.vector.memset(ones[:, :], 1.0))
            nc.vector.tensor_reduce(sel[:, :, :], hot[:, :, :, :].rearrange("p t k e -> p t e k"), axis=AX.X,
                                    op=ALU.add).then_inc(sel_ready, 1)
            dve.wait_ge(soft_out, 1)
            link(nc.vector.tensor_reduce(wsum[:, :], weight[:, :, :], axis=AX.X, op=ALU.add))
            link(nc.vector.reciprocal(wsum[:, :], wsum[:, :]))
            link(nc.vector.tensor_tensor(weight[:, :, :], weight[:, :, :],
                                         wsum[:, :].rearrange("p (t o) -> p t o", o=1).to_broadcast([P, NT, K]), ALU.mult))
            dve.wait_ge(ranked, 1)
            link(nc.vector.tensor_copy(tot[:, :, :], bank[1][:, 0:NT * E].rearrange("p (t e) -> p e t", t=NT)))
            link(nc.vector.tensor_tensor_scan(cum[:, :, :].rearrange("p e t -> p (e t)"), const(ca, CA, "carry"),
                                              tot[:, :, :].rearrange("p e t -> p (e t)"), 0.0, ALU.mult, ALU.add))
            link(nc.vector.tensor_scalar(cnt[:, :], cum[:, :, NT - 1], float(P - 1), None, ALU.add))
            link(nc.vector.tensor_copy(nt_i[:, :], cnt[:, :]))
            link(nc.vector.tensor_scalar(nt_i[:, :], nt_i[:, :], 7, None, ALU.logical_shift_right))
            link(nc.vector.tensor_copy(nt_f[:, :], nt_i[:, :]))
            link(nc.vector.tensor_tensor_scan(ends[:, :], ones[:, 0:E], nt_f[:, :], 0.0, ALU.mult, ALU.add))
            link(nc.vector.tensor_tensor(nt_f[:, :], ends[:, :], nt_f[:, :], ALU.subtract))
            link(nc.vector.tensor_tensor(cum[:, :, :], cum[:, :, :], tot[:, :, :], ALU.subtract))
            link(nc.vector.tensor_scalar(nt_f[:, :], nt_f[:, :], float(P), None, ALU.mult))
            link(nc.vector.tensor_tensor(cum[:, :, :], cum[:, :, :], nt_f[:, :].rearrange("p (e o) -> p e o", o=1).to_broadcast([P, E, NT]), ALU.add))
            link(nc.vector.tensor_tensor(sel[:, :, :], cum[:, :, :].rearrange("p e t -> p t e"),
                                         bank[0][:, 0:NT * E].rearrange("p (t e) -> p t e", t=NT), ALU.add))
            link(nc.vector.tensor_tensor(hot[:, :, :, :], hot[:, :, :, :],
                                         sel[:, :, :].rearrange("p t (o e) -> p t o e", o=1).to_broadcast([P, NT, K, E]), ALU.mult))
            link(nc.vector.tensor_reduce(pos[:, :], hot[:, :, :, :].rearrange("p t k e -> p (t k) e"), axis=AX.X, op=ALU.add))
            link(nc.vector.tensor_copy(pos_i[:, :], pos[:, :]))
            link(nc.vector.tensor_scalar(topi[:, :, :].rearrange("p t k -> p (t k)")[:, 0:NT * K].bitcast(I32), pos_i[:, :], 7, None,
                                         ALU.logical_shift_right))
            link(nc.vector.tensor_scalar(pos_i[:, :], pos_i[:, :], P - 1, None, ALU.bitwise_and))
            link(nc.vector.tensor_copy(jf[:, :], topi[:, :, :].rearrange("p t k -> p (t k)")[:, 0:NT * K].bitcast(I32)))
            link(nc.vector.tensor_copy(rf[:, :], pos_i[:, :]))

            dest_c = const(ca, CA, "dest")
            iota_p = const(ca, CA, "iota_p")
            iota_j = const(ca, CA, "iota_j")
            with dve.Fori(0, NT * K // 2) as i:
                for q in range(2):
                    c = ds(2 * i + q, 1)
                    dve.wait_ge(pair_used[q], i)
                    nc.vector.tensor_scalar(onehot_p[q][:, :], iota_p, rf[:, c], None, ALU.is_equal)
                    nc.vector.tensor_scalar(onehot_j[q][:, :], iota_j, jf[:, c], dest_c[:, c],
                                            ALU.is_equal, ALU.mult).then_inc(pair_ready[q], 1)
            link(nc.vector.tensor_tensor(cmp_j[:, :, :], ends[0:1, :].rearrange("p (o e) -> p o e", o=1).to_broadcast([1, NS, E]),
                                         iota_j[0:1, :].rearrange("p (j o) -> p j o", o=1).to_broadcast([1, NS, E]), ALU.is_le))
            link(nc.vector.tensor_reduce(te_f[:, :], cmp_j[:, :, :], axis=AX.X, op=ALU.add))
            link(nc.vector.tensor_scalar(te_f[:, :], te_f[:, :], float(E - 1), None, ALU.min))
            link(nc.vector.tensor_copy(te_i[:, :], te_f[:, :]))
            dve.wait_ge(inverse_done, 1)
            link(nc.vector.scalar_tensor_tensor(pad_f[:, :], bank[3][:, 0:NS], 0.0, const(ca, CA, "trash"), ALU.is_equal, ALU.mult))
            link(nc.vector.scalar_tensor_tensor(dest_f[:, :], bank[3][:, 0:NS], -1.0, pad_f[:, :], ALU.add, ALU.add))
            link(nc.vector.tensor_copy(dest_i[:, :], dest_f[:, :]))
            link(nc.vector.tensor_scalar(dest_f[:, :], dest_f[:, :], const(ca, CA, "pad_row"), None, ALU.min))
            link(nc.vector.tensor_copy(tok_i[:, :], dest_f[:, :]))
            link(nc.vector.tensor_scalar(tok_hi[:, :], tok_i[:, :], 9, 7, ALU.logical_shift_right, ALU.logical_shift_left))
            link(nc.vector.tensor_scalar(tok_lo[:, :], tok_i[:, :], P - 1, None, ALU.bitwise_and))
            nc.vector.tensor_tensor(tok_i[:, :], tok_hi[:, :], tok_lo[:, :], ALU.bitwise_or).then_inc(lists_ready, 1)
            dve.wait_ge(lists_ready, 1)

            def rows_in(j):
                p, n = j
                dve.wait_ge(gathered[p], n * DMA)
                nc.vector.tensor_scalar(idx_in[p][:, :], tok_i[:, ds(2 * n + p, 1)], 0.0, None, ALU.add).then_inc(in_idx[p], 1)

            def step(j, at):
                if has(at, 2):
                    p, n = of(j, 2)
                    dve.wait_ge(xh_ready[p], n + 1)
                    nc.vector.tensor_tensor(xl[p][:, :, :], bank[p][:, 0:D].rearrange("p (c n) -> p c n", c=DC),
                                            xh[p][:, :, :].bitcast(F32), ALU.subtract).then_inc(xl_ready[p], 1)
                if has(at, 4):
                    rows_in(of(j, 4))
                if has(at, 1):
                    p, n = of(j, 1)
                    dve.wait_ge(sg_ready[p], n + 1)
                    dve.wait_ge(av_turned[p], n)
                    nc.vector.tensor_tensor(av[p][:, :], bank[2 + p][:, I:2 * I], sg[p][:, :], ALU.mult).then_inc(av_ready[p], 1)
                if has(at, 0):
                    p, n = j
                    dve.wait_ge(ah_ready[p], n + 1)
                    nc.vector.tensor_tensor(al[p][:, :, :], bank[4 + p][0:IH, 0:2 * P].rearrange("p (c n) -> p c n", c=2),
                                            ah[p][:, :, :].bitcast(F32), ALU.subtract).then_inc(al_ready[p], 1)
                if has(at, -1):
                    p, n = of(j, -1)
                    dve.wait_ge(scattered[p], n * DMA)
                    nc.vector.tensor_scalar(idx_out[p][:, :], dest_i[:, ds(2 * n + p, 1)], 0.0, None, ALU.add).then_inc(out_idx[p], 1)

            rows_in((0, 0))
            rows_in((1, 0))
            for j in (-2, -1, 0):
                step((j % 2, j // 2), j)
            with dve.Fori(0, LOOP - 1) as i:
                step((1, i), None)
                step((0, i + 1), None)
            for j in range(NS - 4, NS + 1):
                step((j % 2, j // 2), j)

            dve.wait_ge(rep_ready, 1)
            dve.wait_ge(wo_in, 3 * DMA)
            link(nc.vector.tensor_tensor(hmask[:, :], const(cc, CC, "heads"), lscale[:, :], ALU.mult))
            pmask = const(cc, CC, "pair")
            nc.vector.memset(vb[:, :, :, :], 0.0).then_inc(set_dve, 1)
            dve.wait_ge(set_dve, 1)
            n_set = 1
            n_rep = 0
            for b in range(NB):
                dve.wait_ge(set_pe, 2 + 4 * b)
                for g in range(HKV):
                    hm = hmask[:, g * G:(g + 1) * G].rearrange("p (h o) -> p h o", o=1).to_broadcast([P, G, NKEY])
                    for bd, at in ((bd_s, 0), (bd_g, NKEY)):
                        kv = bank[4 + g][:, at:at + NKEY].rearrange("p (o k) -> p o k", o=1).to_broadcast([P, G, NKEY])
                        last = nc.vector.tensor_tensor(bd[:, b, g, :, :], kv, hm, ALU.mult)
                last.then_inc(set_dve, 1)
                dve.wait_ge(set_pe, 4 + 4 * b)
                for g in range(HKV):
                    rep = bank[4 + g]
                    for m in range(2):
                        pr_n = 2 * g + m
                        col = 2 * (pr_n % 4) * NBLK
                        nc.vector.tensor_tensor(
                            vb[:, b, pr_n, col:col + 2 * NBLK].rearrange("p (h k) -> p h k", h=2),
                            rep[:, 0:NBLK].rearrange("p (o k) -> p o k", o=1).to_broadcast([P, 2, NBLK]),
                            pmask.rearrange("p (h o) -> p h o", o=1).to_broadcast([P, 2, NBLK]), ALU.mult)
                        last = nc.vector.tensor_reduce(vb[:, b, pr_n if pr_n >= 4 else 8 + pr_n, HALF:HALF + 1],
                                                       rep[:, NBLK:NKEY], axis=AX.X, op=ALU.add)
                last.then_inc(set_dve, 1)

            cosq, sinq = cos, sin

            def rope_q(i, u):
                dve.wait_ge(c_q[u], i + 1)
                dve.wait_ge(c_qr[u], i)
                raw = bank[2 + u][:, :].rearrange("p (g h d) -> p g h d", g=H, h=2)
                r2 = q2[u][:, :, :].rearrange("p g (h d) -> p g h d", h=2)
                co = cosq[:, ds(i * DS, DS)].rearrange("p (o d) -> p o d", o=1).to_broadcast([P, H, DS])
                s_lo = sinq[:, ds(i * DS, DS // 2)].rearrange("p (o d) -> p o d", o=1).to_broadcast([P, H, DS // 2])
                s_hi = sinq[:, ds(i * DS + DS // 2, DS // 2)].rearrange("p (o d) -> p o d", o=1).to_broadcast([P, H, DS // 2])
                nc.vector.tensor_tensor(q1[u][:, :, :], bank[2 + u][:, :].rearrange("p (g d) -> p g d", g=H), co, ALU.mult)
                nc.vector.tensor_tensor(r2[:, :, 0, :], raw[:, :, 1, :], s_lo, ALU.mult)
                nc.vector.tensor_tensor(r2[:, :, 1, :], raw[:, :, 0, :], s_hi, ALU.mult).then_inc(c_roped[u], 1)

            LINKS = 6

            def tile_link(ins, i, u, k):
                ins.then_inc(c_link[u], 1)
                dve.wait_ge(c_link[u], i * LINKS + k)

            def sum_link(ins, i, u, k):
                ins.then_inc(c_sum[u], 1)
                dve.wait_ge(c_sum[u], i * K + k)

            def over_keys(v, n=H, k=NBLK):
                return v.rearrange("p (h o) -> p h o", o=1).to_broadcast([P, n, k])

            def scores(i, u):
                see = const(cc, CC, "see")[:, ds(i * NBLK, NBLK)].rearrange("p (o k) -> p o k", o=1).to_broadcast([P, H, NBLK])
                hide = const(cc, CC, "hide")[:, ds(i * NBLK, NBLK)].rearrange("p (o k) -> p o k", o=1).to_broadcast([P, H, NBLK])
                dve.wait_ge(c_s[u], i + 1)
                tile_link(nc.vector.tensor_tensor(s1[u][:, :, :], bank[6 + u][:, 0:HK].rearrange("p (h k) -> p h k", h=H), see, ALU.mult), i, u, 1)
                tile_link(nc.vector.tensor_tensor(s2[u][:, :, :], s1[u][:, :, :], hide, ALU.add), i, u, 2)
                tile_link(nc.vector.tensor_reduce(smax[u][:, :], s2[u][:, :, :], axis=AX.X, op=ALU.max), i, u, 3)
                dve.wait_ge(c_ex[u], i)
                nc.vector.tensor_tensor(sd[u][:, :, :], s2[u][:, :, :], over_keys(smax[u][:, :]), ALU.subtract).then_inc(c_d[u], 1)

            def probabilities(i, u):
                dve.wait_ge(c_ex[u], i + 1)
                dve.wait_ge(c_pt[u], i)
                tile_link(nc.vector.tensor_reduce(ssum[u][:, :], ex[u][:, :, :], axis=AX.X, op=ALU.add), i, u, 4)
                tile_link(nc.vector.tensor_scalar(sfull[u][:, :], ssum[u][:, :], const(cc, CC, "more")[:, ds(i, 1)], None, ALU.add), i, u, 5)
                tile_link(nc.vector.reciprocal(srec[u][:, :], sfull[u][:, :]), i, u, 6)
                nc.vector.tensor_scalar(pr[u][:, HK:HK + 1], const(cc, CC, "even")[:, ds(i, 1)], 1.0, None, ALU.mult)
                nc.vector.tensor_tensor(pr[u][:, 0:HK].rearrange("p (h k) -> p h k", h=H), ex[u][:, :, :],
                                        over_keys(srec[u][:, :]), ALU.mult).then_inc(c_p[u], 1)

            def add_up(i, u):
                t = u * TB + i
                dve.wait_ge(c_o[u], i + 1)
                dve.wait_ge(xr_in[u], (i + 1) * DMA)
                dve.wait_ge(yv_in[u], (i + 1) * DMA)
                dve.wait_ge(c_stored[u], i * DMA)
                sum_link(nc.vector.tensor_tensor(acc[u][0][:, :], bank[2 + u][:, 0:D], xr[u][:, :], ALU.add), i, u, 1)
                w_all = weight[:, :, :].rearrange("p t k -> p (t k)")
                for k in range(K):
                    ins = nc.vector.scalar_tensor_tensor(acc[u][k + 1][:, :], yv[u][:, k, :], w_all[:, ds(t * K + k, 1)],
                                                         acc[u][k][:, :], ALU.mult, ALU.add)
                    if k < K - 1:
                        sum_link(ins, i, u, 2 + k)
                    else:
                        ins.then_inc(c_out[u], 1)

            with dve.Fori(0, REMOTE) as i:
                for stage_c in (rope_q, scores, probabilities, add_up):
                    for u in range(NB):
                        stage_c(i, u)

            see_l = const(cc, CC, "see_l")
            hide_l = const(cc, CC, "hide_l")
            n_pe = 0
            n_act = 0
            for u in range(NB):
                rope_q(REMOTE, u)
                n_pe += 2
                n_act += 2
                if u:
                    dve.wait_ge(c_pt[0], TB)
                link(nc.vector.tensor_copy(pr[u][:, HK:HK + 1], const(cc, CC, "even")[:, TB - 1:TB]))
                for g in range(HKV):
                    n_pe += 1
                    dve.wait_ge(l_pe, n_pe)
                    for m in range(2):
                        last = nc.vector.tensor_tensor(
                            l1[:, 2 * m:2 * m + 2, :], bank[2 * m + (1 - u)][:, 0:2 * NKEY].rearrange("p (h k) -> p h k", h=2),
                            see_l.rearrange("p (o k) -> p o k", o=1).to_broadcast([P, 2, NKEY]), ALU.mult)
                    last.then_inc(l_dve, 1)
                    dve.wait_ge(l_dve, (u * HKV + g) * 3 + 1)
                    link(nc.vector.tensor_tensor(l2[:, :, :], l1[:, :, :], hide_l.rearrange("p (o k) -> p o k", o=1).to_broadcast([P, G, NKEY]), ALU.add))
                    link(nc.vector.tensor_reduce(lmax[:, :], l2[:, :, :], axis=AX.X, op=ALU.max))
                    nc.vector.tensor_tensor(l3[:, :, :], l2[:, :, :], over_keys(lmax[:, :], G, NKEY), ALU.subtract).then_inc(l_dve, 1)
                    n_act += 1
                    dve.wait_ge(l_act, n_act)
                    link(nc.vector.tensor_reduce(lsum[:, :], lex[:, :, :], axis=AX.X, op=ALU.add))
                    link(nc.vector.reciprocal(lrec[:, :], lsum[:, :]))
                    last = nc.vector.tensor_tensor(pr[u][:, g * G * NBLK:(g + 1) * G * NBLK].rearrange("p (h k) -> p h k", h=G),
                                                   lex[:, :, 0:NBLK], over_keys(lrec[:, :], G, NBLK), ALU.mult)
                    if g == HKV - 1:
                        last.then_inc(c_p[u], 1)
                    nc.vector.tensor_tensor(lp[g % 2][:, :, :], lex[:, :, NBLK:NKEY], over_keys(lrec[:, :], G, LW), ALU.mult).then_inc(l_dve, 1)
                    n_pe += 2
                    n_act += 2
                n_pe += 1
                n_act += 1
                add_up(REMOTE, u)

        @block.tensor
        def _(pe):
            def mm(o, lhsT, rhs, start, stop):
                return nc.tensor.matmul(o, lhsT, rhs, start=start, stop=stop)

            pe.wait_ge(const_in, 3 * DMA)
            for c in range(DC):
                last = nc.tensor.transpose(bank[7][:, c * E:(c + 1) * E], rw[:, c * P:(c + 1) * P], ident[0:E, 0:E])
            last.then_inc(rw_t, 1)
            pe.wait_ge(rwT_ready, 1)

            def turn(i, u):
                pe.wait_ge(xn_ready[u], i + 1)
                pe.wait_ge(xT_ready[u], i)
                for c in range(DC):
                    last = nc.tensor.transpose(bank[u][:, c * P:(c + 1) * P], xnb[u][:, c * P:(c + 1) * P], ident)
                last.then_inc(xn_turned[u], 1)

            def project(i, u):
                pe.wait_ge(xT_ready[u], i + 1)
                pe.wait_ge(krot_ready[u], i)
                for c in range(DC):
                    mm(bank[2][:, ds((u * TB + i) * E, E)], xT[u][:, c, :], rwT[:, c, :], c == 0, c == DC - 1)
                for c in range(DC):
                    last = mm(bank[3 + u][:, 0:HKV * DS], xT[u][:, c, :], wkg[:, c, :], c == 0, c == DC - 1)
                last.then_inc(k_raw[u], 1)

            def block_means(i, u):
                for c in range(DC):
                    mm(bank[5 + u][:, ds(NBLK * (1 + c) + 2 * i, 2)], xnb[u][:, c * P:(c + 1) * P], pool2, True, True)
                pe.wait_ge(krot_ready[u], i + 1)
                mm(bank[5 + u][:, ds(2 * i, 2)], krot[u][:, :], pool2, True, True).then_inc(pooled[u], 1)

            with pe.Fori(0, REMOTE) as i:
                for part in (turn, project, block_means):
                    for u in range(NB):
                        part(i, u)
            for u in range(NB):
                turn(REMOTE, u)
            for u in range(NB):
                project(REMOTE, u)
            for u in range(NB):
                pe.wait_ge(krot_ready[u], TB)
                nc.tensor.transpose(bank[5 + u][:, 64:64 + P], krot[u][:, :], ident).then_inc(keys_turned[u], 1)

            pe.wait_ge(sel_ready, 1)
            sel_v = sel[:, :, :].rearrange("p t e -> p (t e)")
            mm(bank[0][:, 0:NT * E], below, sel_v, True, True)
            mm(bank[1][:, 0:NT * E], ones[:, :], sel_v, True, True).then_inc(ranked, 1)
            COLS = NT * K // 2

            def column(i, q, start, stop):
                pe.wait_ge(pair_ready[q], i + 1)
                return mm(bank[3][:, 0:NS], onehot_p[q][:, :], onehot_j[q][:, :], start, stop).then_inc(pair_used[q], 1)

            column(0, 0, True, False)
            column(0, 1, False, False)
            with pe.Fori(1, COLS - 1) as i:
                column(i, 0, False, False)
                column(i, 1, False, False)
            column(COLS - 1, 0, False, False)
            pe.wait_ge(pair_ready[1], COLS)
            mm(bank[3][:, 0:NS], onehot_p[1][:, :], onehot_j[1][:, :], False, True).then_inc(inverse_done, 1)

            for s in range(2):
                pe.wait_ge(w_lo[s], E // 2)
            pe.wait_ge(lists_ready, 1)

            def three(o, hi, lo, w_hi_, w_lo_, at, width, chunks):
                for c in range(chunks):
                    cols = ds(at + c * width, width)
                    mm(o, hi[:, c, :], w_hi_[:, cols], c == 0, False)
                    mm(o, hi[:, c, :], w_lo_[:, cols], False, False)
                    last = mm(o, lo[:, c, :], w_hi_[:, cols], False, c == chunks - 1)
                return last

            def expert(n, p):
                return pe.value_load(te_i[0:1, ds(2 * n + p, 1)], min_val=0, max_val=E - 1)

            def step(j, at):
                if has(at, 2):
                    p, n = of(j, 2)
                    pe.wait_ge(gathered[p], (n + 1) * DMA)
                    pe.wait_ge(xl_ready[p], n)
                    for c in range(DC):
                        last = nc.tensor.transpose(bank[p][:, c * P:(c + 1) * P], xg[p][:, c * P:(c + 1) * P], ident)
                    last.then_inc(x_turned[p], 1)
                if has(at, 1):
                    p, n = of(j, 1)
                    e = expert(n, p)
                    pe.wait_ge(xl_ready[p], n + 1)
                    pe.wait_ge(av_ready[p], n)
                    three(bank[2 + p][:, 0:2 * I], xh[p], xl[p], wgu_h, wgu_l, e * WGU, 2 * I, DC).then_inc(gu_done[p], 1)
                if has(at, 0):
                    p, n = j
                    pe.wait_ge(av_ready[p], n + 1)
                    pe.wait_ge(al_ready[p], n)
                    for c in range(2):
                        last = nc.tensor.transpose(bank[4 + p][0:IH, c * P:(c + 1) * P], av[p][:, c * IH:(c + 1) * IH], ident)
                    last.then_inc(av_turned[p], 1)
                if has(at, -1):
                    p, n = of(j, -1)
                    e = expert(n, p)
                    pe.wait_ge(al_ready[p], n + 1)
                    pe.wait_ge(y_ready[p], n)
                    three(bank[6 + p][:, 0:D], ah[p], al[p], wdn_h, wdn_l, e * WDN, D, 2).then_inc(y_done[p], 1)

            steps(pe, step)

            pe.wait_ge(wc_in, 4 * DMA)
            for p in range(2):
                pe.wait_ge(y_ready[p], TILES[p])
            for g in range(HKV):
                for c in range(DC):
                    last = nc.tensor.transpose(bank[g][:, c * P:(c + 1) * P], wqs[:, c, g * P:(g + 1) * P], ident)
            last.then_inc(set_pe, 1)
            pe.wait_ge(rep_ready, 1)
            copies = const(cc, CC, "copies")
            for b in range(NB):
                if b:
                    pe.wait_ge(set_dve, 3)
                for g in range(HKV):
                    for c in range(DC):
                        mm(bank[4 + g][:, 0:NKEY], wk_rep[:, c, g, :, :].rearrange("p h d -> p (h d)"), x_keys[:, c, b, :], c == 0, c == DC - 1)
                    last = mm(bank[4 + g][:, NKEY:2 * NKEY], copies[:, g * P:(g + 1) * P], kgeo_t[:, b, :], True, True)
                last.then_inc(set_pe, 1)
                pe.wait_ge(set_act, 1 + 2 * b)
                pe.wait_ge(set_dve, 2 + 2 * b)
                for c in range(DC):
                    for g in range(HKV):
                        last = mm(bank[0][:, c * HK + g * G * NBLK:c * HK + (g + 1) * G * NBLK],
                                  wqT[:, g, c * P:(c + 1) * P], bd_s[:, b, g, :, 0:NBLK], True, True)
                last.then_inc(set_pe, 1)
                for g in range(HKV):
                    for c in range(DC):
                        last = mm(bank[4 + g][:, 0:NKEY], wv_rep[:, c, g, :, :].rearrange("p h d -> p (h d)"), x_keys[:, c, b, :], c == 0, c == DC - 1)
                last.then_inc(set_pe, 1)
                pe.wait_ge(set_dve, 3 + 2 * b)
                for n in range(4):
                    mm(bank[1][0:HALF, 0:D], vb[:, b, n, 0:HALF], wo_s[:, n, :], n == 0, n == 3)
                for n in range(8):
                    mm(bank[2][0:HALF + 1, 0:D], vb[:, b, 4 + n, :], wo_s[:, (4 + n) % 8, :], n == 0, n == 7)
                for c in range(DC):
                    last = mm(bank[3][:, 0:HKV * DV], x_keys[:, c, b, NBLK:NKEY], wv_s[:, c, :], c == 0, c == DC - 1)
                last.then_inc(set_pe, 1)
            pe.wait_ge(set_act, 1 + 2 * NB)

            def x_turn(i, u):
                pe.wait_ge(xc_in[u], (i + 1) * DMA)
                pe.wait_ge(c_pT[u], i)
                for c in range(DC):
                    last = nc.tensor.transpose(bank[u][:, c * P:(c + 1) * P], xc[u][:, c * P:(c + 1) * P], ident)
                last.then_inc(c_xt[u], 1)

            def q_project(i, u):
                pe.wait_ge(c_xT[u], i + 1)
                pe.wait_ge(c_out[u], i)
                for c in range(DC):
                    last = mm(bank[2 + u][:, :], xcT[u][:, c, :], wqg[:, c, :], c == 0, c == DC - 1)
                last.then_inc(c_q[u], 1)

            def q_turn(i, u):
                pe.wait_ge(c_qr[u], i + 1)
                pe.wait_ge(c_qT[u], i)
                for g in range(HKV):
                    last = nc.tensor.transpose(bank[4 + u][:, g * P:(g + 1) * P], qr[u][:, g * P:(g + 1) * P], ident)
                last.then_inc(c_qt[u], 1)

            def score(i, u):
                pe.wait_ge(c_qT[u], i + 1)
                pe.wait_ge(c_d[u], i)
                for c in range(DC):
                    mm(bank[6 + u][:, 0:HK], xcT[u][:, c, :], asem[:, u, c, :], c == 0, False)
                for g in range(HKV):
                    last = mm(bank[6 + u][:, g * G * NBLK:(g + 1) * G * NBLK], qrT[u][:, g, :], bd_g[:, u, g, :, 0:NBLK],
                              False, g == HKV - 1)
                last.then_inc(c_s[u], 1)

            def p_turn(i, u):
                pe.wait_ge(c_p[u], i + 1)
                nc.tensor.transpose(bank[u][0:HALF, 0:P], pr[u][:, 0:HALF], ident)
                nc.tensor.transpose(bank[u][0:HALF + 1, P:2 * P], pr[u][:, HALF:HK + 1], ident).then_inc(c_pt[u], 1)

            def attend(i, u):
                pe.wait_ge(c_pT[u], i + 1)
                mm(bank[2 + u][:, 0:D], prT[u][0:HALF, 0, :], vw[0:HALF, u, 0, :], True, False)
                mm(bank[2 + u][:, 0:D], prT[u][:, 1, :], vw[:, u, 1, :], False, True).then_inc(c_o[u], 1)

            with pe.Fori(0, REMOTE) as i:
                for part in (x_turn, q_project, q_turn, score, p_turn, attend):
                    for u in range(NB):
                        part(i, u)

            n_act = 0
            for u in range(NB):
                v = 1 - u
                if u == 0:
                    for w in range(NB):
                        pe.wait_ge(c_out[w], REMOTE)
                        pe.wait_ge(c_d[w], REMOTE)
                else:
                    pe.wait_ge(c_out[0], TB)
                x_turn(REMOTE, u)
                q_project(REMOTE, u)
                for c in range(DC):
                    last = mm(bank[6][:, :], xcT[u][:, c, :], wqs[:, c, :], c == 0, c == DC - 1)
                last.then_inc(l_pe, 1)
                q_turn(REMOTE, u)
                n_act += 1
                pe.wait_ge(l_act, n_act)
                for g in range(HKV):
                    last = nc.tensor.transpose(bank[5 - u][:, g * P:(g + 1) * P], qs[:, g * P:(g + 1) * P], ident)
                last.then_inc(l_pe, 1)
                n_act += 1
                pe.wait_ge(l_act, n_act)
                pe.wait_ge(c_qT[u], TB)
                for g in range(HKV):
                    if g:
                        pe.wait_ge(l_dve, (u * HKV + g) * 3 - 2)
                    for m in range(2):
                        o = bank[2 * m + v][:, 0:2 * NKEY]
                        mm(o, qrT[u][:, g, :], bd_g[:, u, g, 2 * m:2 * m + 2, :].rearrange("p h k -> p (h k)"), True, False)
                        last = mm(o, qsT[:, g, :], bd_s[:, u, g, 2 * m:2 * m + 2, :].rearrange("p h k -> p (h k)"), False, True)
                    last.then_inc(l_pe, 1)
                    n_act += 1
                    pe.wait_ge(l_dve, (u * HKV + g) * 3 + 3)
                    for h in range(G):
                        last = nc.tensor.transpose(bank[7][:, h * P:(h + 1) * P], lp[g % 2][:, h, :], ident)
                    last.then_inc(l_pe, 1)
                    n_act += 1
                    pe.wait_ge(l_act, n_act)
                    for h in range(G):
                        last = mm(bank[6][:, h * DV:(h + 1) * DV], lpT[g % 2][:, h, :], vloc[:, u, g * DV:(g + 1) * DV], True, True)
                    last.then_inc(l_pe, 1)
                    n_act += 1
                    pe.wait_ge(l_act, n_act)
                for n in range(8):
                    last = nc.tensor.transpose(bank[4 + n // 4][:, (n % 4) * P:(n % 4 + 1) * P], osb[:, n * P:(n + 1) * P], ident)
                last.then_inc(l_pe, 1)
                p_turn(REMOTE, u)
                n_act += 1
                pe.wait_ge(l_act, n_act)
                pe.wait_ge(c_pT[u], TB)
                mm(bank[2 + u][:, 0:D], prT[u][0:HALF, 0, :], vw[0:HALF, u, 0, :], True, False)
                mm(bank[2 + u][:, 0:D], prT[u][:, 1, :], vw[:, u, 1, :], False, False)
                for n in range(8):
                    last = mm(bank[2 + u][:, 0:D], oT[:, n, :], wo_s[:, n, :], False, n == 7)
                last.then_inc(c_o[u], 1)


def constants():
    import numpy as np

    f = np.float32
    p = np.arange(P)
    a = np.zeros((P, NCA), f)

    def put(m, table, name, v):
        at, n = table[name]
        m[:, at:at + n] = np.asarray(v, f).reshape(P, n)

    put(a, CA, "ident", np.eye(P))
    put(a, CA, "below", p[:, None] < p[None, :])
    put(a, CA, "pool", np.stack([p < MB, p >= MB], 1) / f(MB))
    inv = (1.0 / np.power(f(10000.0), np.arange(0, DS, 2, dtype=f) / f(DS))).astype(f)
    ang = (np.arange(T, dtype=f)[:, None] * inv).astype(f)
    cos, sin = np.cos(ang).astype(f), np.sin(ang).astype(f)
    tiles = lambda v: v.reshape(TB, P, DS).transpose(1, 0, 2)
    put(a, CA, "cos", tiles(np.concatenate([cos, cos], 1)))
    put(a, CA, "sin", tiles(np.concatenate([-sin, sin], 1)))
    put(a, CA, "iota_e", np.tile(np.arange(E), (P, 1)))
    put(a, CA, "iota_j", np.tile(np.arange(NS), (P, 1)))
    put(a, CA, "iota_p", np.tile(p, (P, 1)))
    put(a, CA, "dest", np.arange(NT * K)[None, :] * P + p[:, None] + 1)
    put(a, CA, "trash", NROW + 1 + np.arange(NS)[None, :] * P + p[:, None])
    put(a, CA, "pad_row", N * K + p)
    put(a, CA, "carry", np.tile(np.arange(NT) > 0, (P, E)))
    c = np.zeros((P, NCC), f)
    put(c, CC, "heads", (p[:, None] // DS == np.arange(H)[None, :] % G) * f(SCALE))
    put(c, CC, "pair", p[:, None] // DV == np.arange(2)[None, :])
    pos = np.arange(TB)[:, None] * P + p[None, :]
    see = (np.arange(NBLK) * MB + MB - 1)[None, None, :] <= pos[:, :, None]
    none = pos.T < MB - 1
    put(c, CC, "see", see.transpose(1, 0, 2))
    put(c, CC, "hide", np.where(see, 0.0, NEG).transpose(1, 0, 2))
    put(c, CC, "more", none * LW)
    put(c, CC, "even", none / f(NKEY))
    see_l = np.concatenate([np.ones((P, NBLK), bool), p[None, :] <= p[:, None]], 1)
    put(c, CC, "see_l", see_l)
    put(c, CC, "hide_l", np.where(see_l, 0.0, NEG))
    put(c, CC, "copies", np.stack([p[:, None] == g * DS + p[None, :] % DS for g in range(HKV)], 1))
    return a, c


INPUTS = ["L0_attn_x", "L0_attn_Wq_sem", "L0_attn_Wk_sem", "L0_attn_Wq_geo", "L0_attn_Wk_geo", "L0_attn_Wv", "L0_attn_Wo",
          "L0_attn_logit_scale", "L0_ffn_router_w", "L0_ffn_expert_bias", "L0_ffn_gate_proj", "L0_ffn_up_proj", "L0_ffn_down_proj"]


def kernel(**inputs):
    import numpy as np
    import concourse.bacc as bacc
    from concourse.bass_utils import run_bass_kernel_spmd

    nc = bacc.Bacc("TRN2", target_bir_lowering=False, num_devices=1, dynamic_dma_scratch_size=8192)
    arrays = {name: np.ascontiguousarray(inputs[name]) for name in INPUTS}
    arrays["const_a"], arrays["const_c"] = constants()
    handles = [nc.dram_tensor(f"in_{name}", a.shape, mybir.dt.from_np(a.dtype), kind="ExternalInput").ap() for name, a in arrays.items()]
    out = nc.dram_tensor("out_rows", (NB, T, D), F32, kind="ExternalOutput").ap()
    build(nc, *handles, out)
    r = run_bass_kernel_spmd(nc, [{f"in_{name}": a for name, a in arrays.items()}], core_ids=[0])
    return r.results[0]["out_rows"]
```

```python
from contextlib import ExitStack

import concourse.bass as bass
from concourse import mybir

F32 = mybir.dt.float32
F32R = mybir.dt.float32r
BF16 = mybir.dt.bfloat16
I32 = mybir.dt.int32
U32 = mybir.dt.uint32
ALU = mybir.AluOpType
ACT = mybir.ActivationFunctionType
AX = mybir.AxisListType

P = 128
NB, T, D = 2, 1024, 256
N = NB * T
TB = T // P
NT = N // P
DC = D // P
H, HKV, DS, DV = 16, 4, 32, 64
RH = DS // 2
G = H // HKV
KD = HKV * DS
MB, LW = 64, 128
NBLK = (T - LW) // MB
NKEY = NBLK + LW
HK = H * NBLK
HALF = HK // 2
E, K, I = 16, 4, 224
IH = I // 2
NS = N * K // P + E - 1
NROW = N * K
EPS = 1e-5
NEG = -1e9
SCALE = 1.0 / float(DS) ** 0.5
DMA = 16

WGU, WDN = DC * 2 * I, 2 * D
WHL = WGU + WDN
REMOTE = TB - 1
EARLY = E - 2 * (REMOTE - 1)
GROUPS, GT = 4, 4
UNITS = NB * HKV
CHUNK = NT * K // UNITS


def columns(*parts):
    at, out = 0, {}
    for name, n in parts:
        out[name] = (at, n)
        at += n
    return out, at


CK, NCK = columns(("ident", P), ("cos", TB * RH), ("sin", TB * DS), ("hide", TB * NBLK), ("any", TB), ("more", TB), ("even", TB))
CA, NCA = columns(("below", P), ("pool", 2), ("iota_e", E), ("iota_j", NS), ("iota_p", P), ("column", NT * K), ("row", 1), ("trash", NS),
                  ("pad_row", 1), ("carry", E * NT))
CC, NCC = columns(("heads", H), ("pair", 2), ("quad", G), ("hide_l", NKEY), ("copies", HKV * P))


def build(nc, x, wq_sem, wk_sem, wq_geo, wk_geo, wv, wo, logit_scale, router_w, expert_bias, gate, up, down,
          const_k, const_a, const_c, out):
    x_rows = x.rearrange("b t d -> (b t) d")
    out_rows = out.rearrange("b t d -> (b t) d")
    xn_d = nc.dram_tensor("xn_rows", (N + P, D), F32, kind="Internal").ap()
    part_d = nc.dram_tensor("attended_rows", (N, D), F32, kind="Internal").ap()
    y_d = nc.dram_tensor("expert_rows", (NROW + NS * P, D), F32, kind="Internal").ap()
    ds = bass.ds

    ctx = ExitStack()
    with ctx:
        base = (nc.sbuf_base + 63) // 64 * 64

        class Region:
            def __init__(self, start, size):
                self.start, self.at, self.end = start, start, start + size

            def take(self, name, shape, dtype=F32):
                size = 2 if dtype == BF16 else 4
                for n in shape[1:]:
                    size *= n
                size = (size + 31) // 32 * 32
                assert self.at + size <= self.end, (name, self.at + size - self.end)
                t = nc.alloc_sbuf_tensor_at(name, list(shape), dtype, offset=self.at)
                self.at += size
                return t

        class Spans:

            def __init__(self, *regions):
                self.regions = regions

            def room(self, size):
                return next(r for r in self.regions if r.at + size <= r.end)

            def take(self, name, shape, dtype=F32):
                size = 4
                for n in shape[1:]:
                    size *= n
                return self.room((size + 31) // 32 * 32).take(name, shape, dtype)

            def block(self, size):
                r = self.room(size)
                r.at += size
                return r.at - size

        KEEP, ATT = 3808, 16384
        LOOP = 229368 // 32 * 32 - base - E * 2 * WHL * 4 - KEEP - ATT
        ctx.enter_context(nc.sbuf_tensor("arena", [P, (229368 - base) // 128 * 32], F32))
        r_exp = Region(base, E * 2 * WHL * 4)
        wgu_h = r_exp.take("wgu_hi", [P, E * WGU], F32R)
        wgu_at = r_exp.at
        wgu_l = r_exp.take("wgu_lo", [P, E * WGU], F32R)
        wgu = Region(wgu_at, E * WGU * 4).take("wgu", [P, E * WGU])
        wdn_h = r_exp.take("wdn_hi", [IH, E * WDN], F32R)
        wdn_at = r_exp.at
        wdn_l = r_exp.take("wdn_lo", [IH, E * WDN], F32R)
        wdn = Region(wdn_at, E * WDN * 4).take("wdn", [IH, E * WDN])
        r_one = Spans(*(Region(at + EARLY * n * 4, (E - EARLY) * n * 4)
                        for at, n in ((base, WGU), (wgu_at, WGU), (wgu_at + E * WGU * 4, WDN), (wdn_at, WDN))))
        r_tail = Region(base, E * 2 * WHL * 4)
        r_keep = Region(r_exp.end, KEEP)
        r_att = [Region(r_keep.end, ATT) for _ in range(2)]
        r_loop = [Region(r_keep.end + ATT, LOOP) for _ in range(2)]

        ck = r_keep.take("const_k", [P, NCK])
        weight = r_keep.take("choice_weight", [P, NT, K])
        dest_i = r_keep.take("dest_i", [P, NS], I32)
        tok_i = r_keep.take("tok_i", [P, NS], I32)
        te_i = r_keep.take("tile_expert", [1, NS], I32)

        wat = r_att[0]
        wqg = wat.take("wqg", [P, DC, H * DS])
        asem = wat.take("asem", [P, NB, DC, HK])
        vw = wat.take("vw", [HALF + 1, NB, 2, D])
        bd_g = wat.take("bd_g", [P, NB, HKV, G, NBLK])
        pr = [wat.take(f"pr{u}", [P, HK + 1]) for u in range(NB)]
        smax = [wat.take(f"smax{u}", [P, H]) for u in range(NB)]
        ssum, srec = (wat.take(n, [P, NB, H]) for n in ("ssum", "srec"))
        wl = r_loop[0]
        xc = [wl.take(f"xc{u}", [P, D]) for u in range(NB)]
        xcT_odd = [wl.take(f"xcT{u}_1", [P, DC, P]) for u in range(NB)]
        q2 = wl.take("q2", [P, H * DS])
        xcT = [(wl.take(f"xcT{u}_0", [P, DC, P]), xcT_odd[u]) for u in range(NB)]
        xr = [wl.take(f"xr{u}", [P, D]) for u in range(NB)]
        q1 = [wl.take(f"q1_{u}", [P, H * DS]) for u in range(NB)]
        qrT = [wl.take(f"qrT{u}", [P, HKV, P]) for u in range(NB)]
        prT = [wl.take(f"prT{u}", [HALF + 1, 2, P]) for u in range(NB)]
        part = r_att[1].take("attended", [P, NT, D])
        wb = r_loop[1]
        idx_in = [wb.take(f"idx_in{s}", [P, 1], I32) for s in range(4)]
        idx_out = [wb.take(f"idx_out{s}", [P, 1], I32) for s in range(4)]
        xg = [wb.take(f"xg{s}", [P, D]) for s in range(4)]
        xh = [wb.take(f"xh{p}", [P, DC, P], F32R) for p in range(2)]
        ysb = [wb.take(f"y{s}", [P, D]) for s in range(4)]
        xl = [wb.take(f"xl{p}", [P, DC, P], F32R) for p in range(2)]
        sg = [wb.take(f"sg{p}", [P, I]) for p in range(2)]
        av = [wb.take(f"act{p}", [P, I]) for p in range(2)]
        ah = [wb.take(f"ah{p}", [IH, 2, P], F32R) for p in range(2)]
        al = [wb.take(f"al{p}", [IH, 2, P], F32R) for p in range(2)]
        yv = [r_tail.take(f"yv{s}", [P, K, D]) for s in range(4)]
        total = r_tail.take("total", [P, NT, D])

        wa = r_one
        S_SIZE = 26112
        s_at = wa.block(S_SIZE)
        ca = wa.take("const_a", [P, NCA])
        cc = wa.take("const_c", [P, NCC])
        x_at = wa.block(NT * D * 4)
        x_all = Region(x_at, NT * D * 4).take("x_all", [P, NT, D])
        xT = [wa.take(f"xT{h}", [P, GT, DC, P]) for h in range(2)]
        rope1 = [wa.take(f"rope1_{h}", [P, 2, NB, KD]) for h in range(2)]
        rope2 = [wa.take(f"rope2_{h}", [P, 2, NB, KD]) for h in range(2)]
        x_sum = wa.take("x_sum", [P, NB, DC, 2 * TB])
        wkr = wa.take("wkr", [P, DC, KD + E])
        rw = wa.take("router_rows", [E, D])
        ebias = wa.take("ebias", [P, E])
        stats = wa.take("stats", [P, NT, 6])
        mean, var, dif, rstd, tmp = (wa.take(n, [P, NT]) for n in ("mean", "var", "dif", "rstd", "tmp"))
        zero = wa.take("zero", [P, D])
        x_keys = wa.take("x_keys", [P, DC, NB, NKEY])
        kgeo_t = wa.take("kgeo_t", [P, NB, NKEY])
        logit = wa.take("logit", [P, NT, E])
        top = wa.take("top", [P, NT, 8])
        topi = wa.take("topi", [P, NT, 8], U32)
        topf = wa.take("topf", [P, NT, K])
        sel = wa.take("sel", [P, NT, E])
        tot = wa.take("tot", [P, E, NT])
        cum = wa.take("cum", [P, E, NT])
        cnt, nt_f, ends = (wa.take(n, [P, E]) for n in ("cnt", "nt_f", "ends"))
        nt_i = wa.take("nt_i", [P, E], I32)
        wsum = wa.take("wsum", [P, NT])
        pos = wa.take("pos", [P, NT * K])
        pos_i = wa.take("pos_i", [P, NT * K], I32)
        jf = wa.take("pos_tile", [P, NT * K])
        rf = wa.take("pos_row", [P, NT * K])
        ones = wa.take("ones", [P, P])
        size = CHUNK * (P + 2 * NS) * 2 * 2 + 64
        pair_at = wa.block(size)
        wt = Region(pair_at, size)
        onehot_p = [wt.take(f"onehot_p{q}", [P, CHUNK, P], BF16) for q in range(2)]
        onehot_j = [wt.take(f"onehot_j{q}", [P, CHUNK, 2, NS], BF16) for q in range(2)]
        wt = Region(pair_at, size)
        dest_f = wt.take("dest_f", [P, NS])
        pad_f = wt.take("pad_f", [P, NS])
        tok_lo = wt.take("tok_lo", [P, NS], I32)
        tok_hi = wt.take("tok_hi", [P, NS], I32)
        size = (NS + 1) * E * 4
        hot_at = wa.block(size)
        hot = Region(hot_at, size).take("hot", [P, NT, K, E])
        cmp_j = Region(hot_at, size).take("cmp_j", [1, NS, E])
        te_f = wa.take("te_f", [1, NS])
        wqs = wa.take("wqs", [P, DC, H * DS])
        wv_s = wa.take("wv_s", [P, DC, HKV * DV])
        wks = wa.take("wks", [P, DC, KD])
        wo_s = wa.take("wo_s", [P, H // 2, D])
        lscale = wa.take("lscale", [P, H])
        hmask = wa.take("hmask", [P, H])
        hscale = wa.take("hscale", [P, HKV])
        rep_s = wa.take("rep_s", [P, HKV, NB, NKEY])
        rep_g = wa.take("rep_g", [P, HKV, NB, NKEY])
        vloc = wa.take("vloc", [P, NB, HKV * DV])
        ws = Region(s_at, S_SIZE)
        vb = ws.take("vb", [P, NB, 12, HALF + 1])
        l_at = ws.at
        wk_rep = ws.take("wk_rep", [P, DC, HKV, G, DS])
        wv_rep = ws.take("wv_rep", [P, DC, HKV, 2, DV])
        wqT = ws.take("wqT", [P, HKV, D])
        bd_s = ws.take("bd_s", [P, NB, HKV, G, NBLK])
        vsum = ws.take("vsum", [P, NB, HKV])
        wl = Region(l_at, S_SIZE - (l_at - s_at))
        qsT = [wl.take(f"qsT{u}", [P, HKV, P]) for u in range(NB)]
        l2 = [wl.take(f"l2_{q}", [P, G, NKEY]) for q in range(2)]
        lex = [wl.take(f"lex{q}", [P, G, NKEY]) for q in range(2)]
        lmax = [wl.take(f"lmax{q}", [P, G]) for q in range(2)]
        lneg = [wl.take(f"lneg{q}", [P, G]) for q in range(2)]
        lsum = [wl.take(f"lsum{q}", [P, G]) for q in range(2)]
        lrec = [wl.take(f"lrec{q}", [P, G]) for q in range(4)]
        lpT = [wa.take(f"lpT{q}", [P, G, P]) for q in range(2)]
        wl = Region(x_at, NT * D * 4)
        oT = [wl.take(f"oT{u}", [P, H // 2, P]) for u in range(NB)]
        osb = [wl.take(f"osb{u}", [P, H * DV]) for u in range(NB)]

        bank = [ctx.enter_context(nc.psum_tensor(f"bank{n}", [P, 512], F32)) for n in range(8)]

        def const(t, table, name):
            at, n = table[name]
            return t[:, at:at + n]

        ident, cos, sin = (const(ck, CK, n) for n in ("ident", "cos", "sin"))
        hide, any_key, more, even = (const(ck, CK, n) for n in ("hide", "any", "more", "even"))
        below, pool2 = const(ca, CA, "below"), const(ca, CA, "pool")

        def sem(name):
            return ctx.enter_context(nc.semaphore(name))

        def several(name, n=2):
            return [sem(f"{name}{p}") for p in range(n)]

        const_in, zeros_ready, zero_stored = sem("const_in"), sem("zeros_ready"), sem("zero_stored")
        x_in = several("x_in", 4)
        dve_step, rw_t, rwT_ready, var_ready, std_ready = sem("dve_step"), sem("rw_t"), sem("rwT_ready"), sem("var_ready"), sem("std_ready")
        xn_ready, xn_turned, xT_ready, x_summed = sem("xn_ready"), sem("xn_turned"), sem("xT_ready"), sem("x_summed")
        rope_half, k_raw, rope_done, pooled, xn_stored = sem("rope_half"), sem("k_raw"), sem("rope_done"), sem("pooled"), several("xn_stored")
        keys_turned, keys_kept = sem("keys_turned"), sem("keys_kept")
        w_early, w_late, w_hi, w_lo = sem("w_early"), sem("w_late"), sem("w_hi"), sem("w_lo")
        soft_in, soft_out, sel_ready, ranked = sem("soft_in"), sem("soft_out"), sem("sel_ready"), sem("ranked")
        pair_ready, pair_used = sem("pair_ready"), sem("pair_used")
        inverse_done, lists_ready = sem("inverse_done"), sem("lists_ready")
        kv_in, q_in, hscale_ready, lscale_ready = sem("kv_in"), sem("q_in"), sem("hscale_ready"), sem("lscale_ready")
        wqT_done, rep_done, rep_kept, wv_done = sem("wqT_done"), sem("rep_done"), sem("rep_kept"), sem("wv_done")
        wqT_ready, wrep_ready = sem("wqT_ready"), sem("wrep_ready")
        diagonals_ready = sem("diagonals_ready")
        set_done, set_kept = sem("set_done"), sem("set_kept")
        l_q, l_qs, l_qsT, l_rope, l_qt, l_qT = (sem("l_" + n) for n in ("q_done", "qs_done", "qsT_ready", "roped", "q_turned", "qT_ready"))
        l_read = sem("l_s_read")
        l_s, l_max, l_ex, l_p, l_t, l_pT, l_pv, l_osb = (
            sem("l_" + n) for n in ("s_done", "max_ready", "exp_ready", "p_ready", "turned", "pT_ready", "pv_done", "o_ready"))
        l_ot, l_oT, l_pt, l_prT, l_o = (sem("l_" + n) for n in ("o_turned", "oT_ready", "p_turned", "prT_ready", "all_done"))
        lx_in = sem("lx_in")
        xc_in, xr_in = several("xc_in"), several("xr_in")
        c_xt, c_xT, c_q, c_rope, c_qt, c_qT, c_s, c_d, c_ex, c_p, c_pt, c_pT, c_o, c_out, c_stored, c_rot, c_masked, c_max = (
            several("c_" + n) for n in ("x_turned", "xT_ready", "q_done", "roped", "q_turned", "qT_ready", "s_done", "d_ready", "exp_ready",
                                        "p_ready", "p_turned", "pT_ready", "o_done", "out_ready", "out_stored", "rotated", "masked", "max_ready"))
        c_sum, c_all, c_rec = sem("c_sum_ready"), sem("c_all_ready"), sem("c_rec_ready")
        gathered, scattered = several("gathered", 4), several("scattered", 4)
        in_idx, out_idx, x_turned, xh_ready, xl_ready, gu_done, sg_ready = (
            sem(n) for n in ("in_idx", "out_idx", "x_turned", "xh_ready", "xl_ready", "gu_done", "sg_ready"))
        av_ready, av_turned, ah_ready, al_ready, y_done, y_ready = (
            sem(n) for n in ("av_ready", "av_turned", "ah_ready", "al_ready", "y_done", "y_ready"))
        part_in, yv_in, total_ready, t_link, out_stored = sem("part_in"), several("yv_in", 4), several("total_ready", 4), several("t_link"), sem("out_stored")

        block = ctx.enter_context(nc.Block())

        L_BANKS = (1, 2, 3, 5)

        L_TURNED = ((1, 2), (3, 6))
        L_OUT = (5, 7)

        def rows(dram, t, n=1):
            return dram[ds(t * P, n * P), :]

        def of_expert(w, e):
            width = WGU if w in (wgu, wgu_h, wgu_l) else WDN
            return w[:, ds(e * width, width)]

        def load_expert(eng, e, arrived):
            gate_v = gate.rearrange("e (c p) n -> p e c n", p=P)
            up_v = up.rearrange("e (c p) n -> p e c n", p=P)
            down_v = down.rearrange("e (c p) n -> p e c n", p=IH)
            gu = of_expert(wgu, e).rearrange("p (c n) -> p c n", c=DC)
            dn = of_expert(wdn, e).rearrange("p (c n) -> p c n", c=2)
            eng.dma_start(gu[:, :, 0:I], gate_v[:, ds(e, 1), :, :].rearrange("p o c n -> p (o c) n")).then_inc(arrived, DMA)
            eng.dma_start(gu[:, :, I:2 * I], up_v[:, ds(e, 1), :, :].rearrange("p o c n -> p (o c) n")).then_inc(arrived, DMA)
            eng.dma_start(dn, down_v[:, ds(e, 1), :, :].rearrange("p o c n -> p (o c) n")).then_inc(arrived, DMA)

        class Counts(dict):

            def __init__(self, eng, a, i, dma=False):
                super().__init__()
                self.eng, self.a, self.i, self.dma = eng, a, i, dma

            def __missing__(self, v):
                self[v] = self.eng.to_reg((self.a * self.i + v) * DMA if self.dma else self.a * self.i + v)
                return self[v]

        class Pair:

            def __init__(self, i, off=0, counts=None):
                self.i, self.off, self.counts = i, off, counts

            @property
            def number(self):
                return self.i + self.off

            @property
            def par(self):
                return self.off % 2

            @property
            def first(self):
                return self.counts is None and self.off == 0

            def more(self, k):
                return Pair(self.i, self.off + k, self.counts)

            @property
            def exists(self):
                return self.counts is not None or 0 <= self.off < REMOTE

            def count(self, k):
                return self.counts[self.off + k] if self.counts is not None else self.off + k

        def pairs(eng, body):
            body(Pair(0, 0))
            with eng.Fori(0, (REMOTE - 3) // 2) as r:
                counts = Counts(eng, 2, r)
                for off in (1, 2):
                    body(Pair(2 * r, off, counts))
            for off in range(REMOTE - 2, REMOTE):
                body(Pair(0, off))

        ROUND = 12

        class Tile:

            def __init__(self, i, r, counts=None):
                self.i, self.r, self.counts = i, r, counts

            def __add__(self, d):
                return Tile(self.i, self.r + d, self.counts)

            @property
            def exists(self):
                return self.r >= 0 and (self.counts is not None or self.r < NS)

            @property
            def number(self):
                return self.i * ROUND + self.r

            @property
            def place(self):
                return self.r % 4

            @property
            def par(self):
                return self.r % 2

            @property
            def done(self):
                return self.counts[0][self.r + 1] if self.counts is not None else self.r + 1

            def first_there(self):
                return self.counts is None and self.r < 4

            def dmas(self, more=0):
                lap = self.r // 4 + more
                return self.counts[1][lap] if self.counts is not None else lap * DMA

        def steps(eng, step, rounds):
            for r in range(-2, ROUND + 1):
                step(Tile(0, r))
            with eng.Fori(1, rounds) as i:
                counts = Counts(eng, ROUND, i), Counts(eng, ROUND // 4, i, True)
                for r in range(1, ROUND + 1):
                    step(Tile(i, r, counts))
            for r in range(ROUND * rounds + 1, NS + 1):
                step(Tile(0, r))

        @block.sync
        def _(sp):
            x_v = x.rearrange("b (t p) d -> p b t d", p=P)
            for q in range(GROUPS):
                for b in range(NB):
                    sp.dma_start(x_all[:, :, :].rearrange("p (t b) d -> p t b d", b=NB)[:, 2 * q:2 * q + 2, b, :], x_v[:, b, 2 * q:2 * q + 2, :]).then_inc(x_in[q], DMA)
            by_chunk = lambda w: w.rearrange("(c p) n -> p c n", p=P)
            sp.dma_start(rw[:, :], router_w).then_inc(const_in, DMA)
            sp.dma_start(ck[:, :], const_k).then_inc(const_in, DMA)
            sp.dma_start(wkr[:, :, 0:KD], by_chunk(wk_geo)).then_inc(const_in, DMA)
            sp.dma_start(ca[:, :], const_a).then_inc(const_in, DMA)
            sp.dma_start(wks[:, :, :], by_chunk(wk_sem)).then_inc(kv_in, DMA)
            sp.dma_start(wv_s[:, :, :], by_chunk(wv)).then_inc(kv_in, DMA)
            sp.dma_start(lscale[:, :], logit_scale.rearrange("(a h) -> a h", a=1).to_broadcast([P, H])).then_inc(kv_in, DMA)
            sp.dma_start(cc[:, :], const_c).then_inc(kv_in, DMA)
            sp.dma_start(ebias[:, :], expert_bias.rearrange("(a e) -> a e", a=1).to_broadcast([P, E])).then_inc(kv_in, DMA)
            sp.dma_start(wqs[:, :, :], by_chunk(wq_sem)).then_inc(q_in, DMA)
            sp.dma_start(wqg[:, :, :], by_chunk(wq_geo)).then_inc(q_in, DMA)
            sp.dma_start(wo_s[:, :, :], wo.rearrange("(c p) n -> p c n", p=P)).then_inc(q_in, DMA)
            sp.wait_ge(zeros_ready, 1)
            sp.dma_start(xn_d[N:N + P, :], zero[:, :]).then_inc(zero_stored, DMA)
            for q in range(GROUPS):
                sp.wait_ge(xn_ready, GT * (q + 1))
                sp.dma_start(xn_d[q * GT * P:(q + 1) * GT * P, :].rearrange("(s p) d -> p s d", p=P), x_all[:, q * GT:(q + 1) * GT, :]).then_inc(xn_stored[q % 2], DMA)
            for u in range(NB):
                sp.dma_start(xr[u][:, :], rows(x_rows, u * TB + REMOTE)).then_inc(lx_in, DMA)
            with sp.Fori(0, EARLY) as e:
                load_expert(sp, e, w_early)

            def load_normalised(i, n=None):
                for u in range(NB):
                    if n is not None:
                        sp.wait_ge(c_xt[u], n)
                    sp.dma_start(xc[u][:, :], rows(xn_d, 2 * i + u)).then_inc(xc_in[u], DMA)

            def load_residual(i):
                for u in range(NB):
                    sp.wait_ge(c_stored[u], (i + 1) * DMA)
                    sp.dma_start(xr[u][:, :], rows(x_rows, u * TB + i)).then_inc(xr_in[u], DMA)

            def store_sum(i):
                for u in range(NB):
                    sp.wait_ge(c_out[u], i + 2)
                    sp.dma_start(rows(part_d, 2 * i + u), xr[u][:, :]).then_inc(c_stored[u], DMA)

            def load_pair(i):
                for s in range(2):
                    load_expert(sp, EARLY + 2 * i + s, w_late)

            for h in range(2):
                sp.wait_ge(xn_stored[h], GROUPS // 2 * DMA)
            load_normalised(0)
            load_normalised(1, 1)
            for u in range(NB):
                sp.wait_ge(c_out[u], 1)
                sp.dma_start(part_d[(2 * REMOTE + u) * P:(2 * REMOTE + u + 1) * P, :], xr[u][:, :]).then_inc(c_stored[u], DMA)
            sp.wait_ge(lists_ready, 1)
            sp.wait_ge(zero_stored, DMA)
            load_pair(0)
            load_normalised(2, 2)
            sp.wait_ge(w_hi, EARLY + 2)
            load_pair(1)
            load_residual(0)
            with sp.Fori(1, REMOTE - 2) as i:
                load_normalised(i + 2, i + 2)
                sp.wait_ge(w_hi, EARLY + 2 + 2 * i)
                load_pair(i + 1)
                store_sum(i + -1)
                load_residual(i)
            for i in range(REMOTE - 2, REMOTE):
                store_sum(i - 1)
                load_residual(i)
            store_sum(REMOTE - 1)

            for u in range(NB):
                sp.wait_ge(c_stored[u], TB * DMA)
            sp.dma_start(part[:, :, :], part_d.rearrange("(t p) d -> p t d", p=P)).then_inc(part_in, DMA)

            y_v = y_d.rearrange("(t p) n -> p t n", p=P)
            sp.wait_ge(y_done, NS)
            for s in range(4):
                sp.wait_ge(scattered[s], (NS - s + 3) // 4 * DMA)

            def load_choices(i, s):
                sp.dma_start(yv[s][:, :, :], y_v[:, ds((4 * i + s) * K, K), :]).then_inc(yv_in[s], DMA)

            for s in range(4):
                load_choices(0, s)
            with sp.Fori(1, NT // 4) as i:
                for s in range(4):
                    sp.wait_ge(total_ready[s], i)
                    load_choices(i, s)
            sp.wait_ge(out_stored, NT * DMA)

        @block.gpsimd
        def _(gp):
            nc.gpsimd.memset(zero[:, :], 0.0).then_inc(zeros_ready, 1)
            nc.gpsimd.memset(vb[:, :, :, :], 0.0).then_inc(zeros_ready, 1)

            def split_low(e):
                gp.wait_ge(w_hi, e + 1)
                nc.gpsimd.tensor_tensor(of_expert(wgu_l, e), of_expert(wgu, e), of_expert(wgu_h, e).bitcast(F32), ALU.subtract)
                nc.gpsimd.tensor_tensor(of_expert(wdn_l, e), of_expert(wdn, e), of_expert(wdn_h, e).bitcast(F32), ALU.subtract).then_inc(w_lo, 1)

            with gp.Fori(0, E) as e:
                split_low(e)

            for h in range(2):
                gp.wait_ge(xn_stored[h], GROUPS // 2 * DMA)
            AHEAD = 6

            def gather(s, row_numbers, turned):
                gp.wait_ge(zero_stored, DMA)
                gp.wait_ge(in_idx, row_numbers)
                if turned is not None:
                    gp.wait_ge(x_turned, turned)
                gp.indirect_dma_start(xg[s][:, :], None, xn_d, bass.IndirectOffsetOnAxis(idx_in[s][:, 0:1], 0)).then_inc(gathered[s], DMA)

            def scatter(s, n):
                gp.wait_ge(lists_ready, 1)
                gp.wait_ge(out_idx, n)
                gp.wait_ge(y_ready, n)
                gp.indirect_dma_start(y_d, bass.IndirectOffsetOnAxis(idx_out[s][:, 0:1], 0), ysb[s][:, :], None).then_inc(scattered[s], DMA)

            for t in range(AHEAD):
                gather(t % 4, t + 1, t - 3 if t >= 4 else None)
            LAPS = (NS - AHEAD) // 4
            with gp.Fori(0, LAPS) as i:
                count = [gp.to_reg(4 * i + v) for v in range(1, AHEAD + 5)]
                for r in range(4):
                    gather((r + AHEAD) % 4, count[r + AHEAD], count[r + AHEAD - 4])
                    scatter(r, count[r])
            for k in range(4 * LAPS, NS):
                if k + AHEAD < NS:
                    gather((k + AHEAD) % 4, k + AHEAD + 1, k + AHEAD - 3)
                scatter(k % 4, k + 1)

        @block.scalar
        def _(act):
            act.wait_ge(var_ready, 1)
            nc.scalar.activation(tmp[:, :], var[:, :], ACT.Sqrt).then_inc(std_ready, 1)
            for t in range(TB):
                h, m = t // 2 % 2, t % 2
                act.wait_ge(xn_turned, t + 1)
                if t >= 4:
                    act.wait_ge(k_raw, t - 3)
                    act.wait_ge(x_summed, t - 3)
                nc.scalar.copy(xT[h][:, 2 * m:2 * m + 2, :, :], bank[t % 3][:, :].rearrange("p (s c n) -> p s c n", s=2, c=DC)).then_inc(xT_ready, 1)
                if t == TB // 2:
                    act.wait_ge(kv_in, 5 * DMA)
                    for c in range(DC):
                        for n in range(G):
                            nc.scalar.copy(wk_rep[:, c, :, n, :], wks[:, c, :].rearrange("p (g d) -> p g d", g=HKV))
                        for n in range(2):
                            last = nc.scalar.copy(wv_rep[:, c, :, n, :], wv_s[:, c, :].rearrange("p (g d) -> p g d", g=HKV))
                    last.then_inc(wrep_ready, 1)
                    nc.scalar.activation(lscale[:, :], lscale[:, :], ACT.Exp).then_inc(lscale_ready, 1)

            act.wait_ge(keys_turned, 1)
            act.wait_ge(x_summed, TB)
            for b in range(NB):
                nc.scalar.copy(kgeo_t[:, b, 0:NBLK], bank[7][:, b * 2 * TB:b * 2 * TB + NBLK])
                nc.scalar.copy(kgeo_t[:, b, NBLK:NKEY], bank[7][:, (1 + b) * P:(2 + b) * P])
                nc.scalar.activation(x_keys[:, :, b, 0:NBLK], x_sum[:, b, :, 0:NBLK], ACT.Copy, scale=1.0 / MB)
                last = nc.scalar.copy(x_keys[:, :, b, NBLK:NKEY], xT[1][:, 2 + b, :, :])
            last.then_inc(keys_kept, 1)

            act.wait_ge(wqT_done, 1)
            for m in range(2):
                last = nc.scalar.copy(wqT[:, 2 * m:2 * m + 2, :], bank[2 + m][:, :].rearrange("p (g n) -> p g n", g=2))
            last.then_inc(wqT_ready, 1)
            act.wait_ge(soft_in, 1)
            nc.scalar.activation(weight[:, :, :], weight[:, :, :], ACT.Exp).then_inc(soft_out, 1)
            act.wait_ge(hscale_ready, 1)
            for n in range(2 * HKV):
                g = n % HKV
                act.wait_ge(rep_done, n + 1)
                nc.scalar.activation((rep_s if n < HKV else rep_g)[:, g, :, :], bank[(5, 6, 2, 3)[n % 4]][:, 0:NB * NKEY].rearrange("p (b k) -> p b k", b=NB),
                                     ACT.Copy, scale=hscale[:, g:g + 1]).then_inc(rep_kept, 1)
            for b in range(NB):
                act.wait_ge(set_done, b + 1)
                nc.scalar.copy(asem[:, b, :, :], bank[5 + b][:, 0:DC * HK].rearrange("p (c n) -> p c n", c=DC)).then_inc(set_kept, 1)
            act.wait_ge(set_done, NB + 1)
            nc.scalar.copy(vloc[:, :, :], bank[1][:, :].rearrange("p (b n) -> p b n", b=NB)).then_inc(set_kept, 1)

            def split_high(e):
                nc.scalar.copy(of_expert(wgu_h, e), of_expert(wgu, e))
                nc.scalar.copy(of_expert(wdn_h, e), of_expert(wdn, e)).then_inc(w_hi, 1)

            for u in range(NB):
                act.wait_ge(l_qs, u + 1)
                nc.scalar.copy(qsT[u][:, :, :], bank[6 + u][:, :].rearrange("p (g n) -> p g n", g=HKV)).then_inc(l_qsT, 1)
            for u in range(NB):
                act.wait_ge(l_qt, u + 1)
                nc.scalar.copy(qrT[u][:, :, :], bank[(5, 3)[u]][:, :].rearrange("p (g n) -> p g n", g=HKV)).then_inc(l_qT, 1)

            def l_exp(n):
                q = n % 2
                act.wait_ge(l_max, n + 1)
                if n >= 2:
                    act.wait_ge(l_t, n - 1)
                    act.wait_ge(l_p, n - 1)
                for h in range(G):
                    last = nc.scalar.activation(lex[q][:, h, :], l2[q][:, h, :], ACT.Exp, bias=lneg[q][:, h:h + 1], accum_out=lsum[q][:, h:h + 1])
                last.then_inc(l_ex, 1)

            def l_keep(n):
                act.wait_ge(l_t, n + 1)
                if n >= 2:
                    act.wait_ge(l_pv, n - 1)
                nc.scalar.copy(lpT[n % 2][:, :, :], bank[6][:, :].rearrange("p (h n) -> p h n", h=G)).then_inc(l_pT, 1)

            def keep_values(b):
                act.wait_ge(set_done, NB + 2 + b)
                nc.scalar.copy(vw[0:HALF, b, 0, :], bank[4][0:HALF, 0:D])
                nc.scalar.copy(vw[:, b, 1, :], bank[4][0:HALF + 1, D:2 * D]).then_inc(set_kept, 1)

            for h in range(2):
                act.wait_ge(xn_stored[h], GROUPS // 2 * DMA)
            act.wait_ge(w_early, EARLY * 3 * DMA)
            for n in range(UNITS):
                l_exp(n)
                if n < EARLY:
                    split_high(n)
                if n % HKV == HKV - 1:
                    keep_values(n // HKV)
                l_keep(n)
            for u in range(NB):
                act.wait_ge(l_ot, u + 1)
                for m in range(2):
                    last = nc.scalar.copy(oT[u][:, 4 * m:4 * m + 4, :], bank[L_TURNED[u][m]][:, :].rearrange("p (h n) -> p h n", h=4))
                last.then_inc(l_oT, 1)
                act.wait_ge(l_pt, u + 1)
                nc.scalar.copy(prT[u][0:HALF, 0, :], bank[4][0:HALF, 0:P])
                nc.scalar.copy(prT[u][:, 1, :], bank[4][0:HALF + 1, P:D]).then_inc(l_prT, 1)

            def x_keep(u, t):
                act.wait_ge(c_xt[u], t.count(1))
                nc.scalar.copy(xcT[u][t.par][:, :, :], bank[u][:, 0:D].rearrange("p (c n) -> p c n", c=DC)).then_inc(c_xT[u], 1)

            def p_keep(u, t):
                act.wait_ge(c_pt[u], t.count(1))
                nc.scalar.copy(prT[u][0:HALF, 0, :], bank[u][0:HALF, D:D + P])
                nc.scalar.copy(prT[u][:, 1, :], bank[u][0:HALF + 1, D + P:2 * D]).then_inc(c_pT[u], 1)

            def attention_act(t):
                for u in range(NB):
                    act.wait_ge(c_qt[u], t.count(1))
                    nc.scalar.copy(qrT[u][:, :, :], bank[4 + u][:, :].rearrange("p (g n) -> p g n", g=HKV)).then_inc(c_qT[u], 1)
                pair_left = t.counts is not None or t.off < REMOTE - 1
                if pair_left:
                    act.wait_ge(w_late, (t.number + 1) * 6 * DMA)
                    split_high(EARLY + 2 * t.number)
                if not t.first:
                    for u in range(NB):
                        p_keep(u, t.more(-1))
                for u in range(NB):
                    act.wait_ge(c_d[u], t.count(1))
                    nc.scalar.activation(pr[u][:, 0:HK], pr[u][:, 0:HK], ACT.Exp).then_inc(c_ex[u], 1)
                    if u == 0 and pair_left:
                        split_high(EARLY + 1 + 2 * t.number)
                if t.more(2).exists:
                    for u in range(NB):
                        x_keep(u, t.more(2))

            for n in range(2):
                for u in range(NB):
                    x_keep(u, Pair(0, n))
            pairs(act, attention_act)
            nc.scalar.activation(sg[0][:, 0:1], ident[:, 0:1], ACT.Silu)
            for u in range(NB):
                p_keep(u, Pair(0, REMOTE - 1))

            def step(j):
                t = j + 2
                if t.exists:
                    act.wait_ge(x_turned, t.done)
                    nc.scalar.copy(xh[t.par][:, :, :], bank[t.par][:, 0:D].rearrange("p (c n) -> p c n", c=DC)).then_inc(xh_ready, 1)
                t = j + 1
                if t.exists:
                    act.wait_ge(gu_done, t.done)
                    nc.scalar.activation(sg[t.par][:, :], bank[2 + t.par][:, 0:I], ACT.Silu).then_inc(sg_ready, 1)
                t = j
                if t.exists:
                    act.wait_ge(av_turned, t.done)
                    nc.scalar.copy(ah[t.par][:, :, :], bank[4 + t.par][0:IH, 0:2 * P].rearrange("p (c n) -> p c n", c=2)).then_inc(ah_ready, 1)
                if j.counts is None and j.r == 0:
                    for u in range(NB):
                        act.wait_ge(c_stored[u], TB * DMA)
                t = j + -1
                if t.exists:
                    act.wait_ge(y_done, t.done)
                    if not t.first_there():
                        act.wait_ge(scattered[t.place], t.dmas())
                    nc.scalar.copy(ysb[t.place][:, :], bank[6 + t.par][:, 0:D]).then_inc(y_ready, 1)

            steps(act, step, (NS - 3) // ROUND)

            with act.Fori(0, NT // 4) as i:
                for s in range(4):
                    act.wait_ge(total_ready[s], i + 1)
                    act.dma_start(rows(out_rows, (s % 2) * TB + 2 * i + s // 2), total[:, :, :].rearrange("p t d -> p (t d)")[:, ds((4 * i + s) * D, D)]).then_inc(out_stored, DMA)

        @block.vector
        def _(dve):
            count = [0]

            def link(ins):
                count[0] += 1
                ins.then_inc(dve_step, 1)
                dve.wait_ge(dve_step, count[0])

            for q in range(GROUPS):
                dve.wait_ge(x_in[q], NB * DMA)
                for z in range(q * GT, (q + 1) * GT):
                    last = nc.vector.bn_stats(stats[:, z, :], x_all[:, z, :])
            link(last)
            link(nc.vector.tensor_tensor(dif[:, :], stats[:, :, 1], stats[:, :, 4], ALU.subtract))
            nc.vector.tensor_tensor(mean[:, :], stats[:, :, 1], stats[:, :, 4], ALU.add)
            nc.vector.tensor_tensor(var[:, :], stats[:, :, 2], stats[:, :, 5], ALU.add)
            link(nc.vector.tensor_tensor(tmp[:, :], dif[:, :], dif[:, :], ALU.mult))
            link(nc.vector.tensor_scalar(var[:, :], var[:, :], 1.0 / D, EPS, ALU.mult, ALU.add))
            nc.vector.scalar_tensor_tensor(var[:, :], tmp[:, :], 0.25, var[:, :], ALU.mult, ALU.add).then_inc(var_ready, 1)
            link(nc.vector.tensor_scalar(mean[:, :], mean[:, :], 0.5, None, ALU.mult))
            dve.wait_ge(var_ready, 1)
            dve.wait_ge(std_ready, 1)
            link(nc.vector.reciprocal(rstd[:, :], tmp[:, :]))
            link(nc.vector.tensor_tensor(dif[:, :], rstd[:, :], rstd[:, :], ALU.mult))
            link(nc.vector.tensor_tensor(dif[:, :], dif[:, :], var[:, :], ALU.mult))
            link(nc.vector.tensor_scalar(dif[:, :], dif[:, :], -0.5, 1.5, ALU.mult, ALU.add))
            link(nc.vector.tensor_tensor(rstd[:, :], rstd[:, :], dif[:, :], ALU.mult))

            def normalise(q):
                for z in range(q * GT, (q + 1) * GT):
                    nc.vector.tensor_scalar(x_all[:, z, :], x_all[:, z, :], mean[:, z:z + 1], rstd[:, z:z + 1],
                                            ALU.subtract, ALU.mult).then_inc(xn_ready, 1)

            def over_heads(v, n):
                return v.rearrange("p (o d) -> p o d", o=1).to_broadcast([P, n, RH])

            def keys_and_logits(t):
                h, m = t // 2 % 2, t % 2
                raw = bank[3 + t % 4][:, 0:NB * (KD + E)].rearrange("p (b n) -> p b n", b=NB)
                dve.wait_ge(k_raw, t + 1)
                if t >= 4:
                    dve.wait_ge(pooled, t - 3)
                for b in range(NB):
                    keys = raw[:, b, 0:KD]
                    t1, t2 = rope1[h][:, m, b, :], rope2[h][:, m, b, :]
                    nc.vector.tensor_tensor(t1.rearrange("p (g d) -> p g d", d=RH), keys.rearrange("p (g d) -> p g d", d=RH),
                                            over_heads(cos[:, t * RH:(t + 1) * RH], 2 * HKV), ALU.mult)
                    for half in range(2):
                        of = lambda v, x: v.rearrange("p (g h d) -> p g h d", g=HKV, h=2)[:, :, x, :]
                        at = t * DS + half * RH
                        last = nc.vector.tensor_tensor(of(t2, half), of(keys, 1 - half), over_heads(sin[:, at:at + RH], HKV), ALU.mult)
                last.then_inc(rope_half, 1)
                nc.vector.tensor_tensor(logit[:, 2 * t:2 * t + 2, :], raw[:, :, KD:KD + E],
                                        ebias[:, :].rearrange("p (o e) -> p o e", o=1).to_broadcast([P, NB, E]), ALU.add)
                dve.wait_ge(xT_ready, t + 1)
                nc.vector.tensor_reduce(x_sum[:, :, :, 2 * t:2 * t + 2], xT[h][:, 2 * m:2 * m + 2, :, :].rearrange("p b c (k n) -> p b c k n", k=2),
                                        axis=AX.X, op=ALU.add).then_inc(x_summed, 1)
                dve.wait_ge(rope_half, t + 1)
                nc.vector.tensor_tensor(rope1[h][:, m, :, :], rope1[h][:, m, :, :], rope2[h][:, m, :, :], ALU.add).then_inc(rope_done, 1)

            normalise(0)
            dve.wait_ge(rw_t, 1)
            nc.vector.tensor_copy(wkr[:, :, KD:KD + E], bank[6][:, 0:DC * E].rearrange("p (c n) -> p c n", c=DC)).then_inc(rwT_ready, 1)
            normalise(1)
            dve.wait_ge(const_in, 4 * DMA)
            dve.wait_ge(kv_in, 5 * DMA)
            for q in range(GROUPS):
                if q + 2 < GROUPS:
                    normalise(q + 2)
                for m in range(2):
                    keys_and_logits(2 * q + m)

            dve.wait_ge(lscale_ready, 1)
            link(nc.vector.tensor_tensor(hmask[:, :], const(cc, CC, "heads"), lscale[:, :], ALU.mult))
            nc.vector.tensor_reduce(hscale[:, :], hmask[:, :].rearrange("p (g h) -> p g h", g=HKV), axis=AX.X, op=ALU.add).then_inc(hscale_ready, 1)

            dve.wait_ge(x_summed, TB)
            for t in range(NT):
                last = nc.vector.max(top[:, t, :], logit[:, t, :])
            link(last)
            nc.vector.tensor_tensor(weight[:, :, :], top[:, :, 0:K], top[:, :, 0:1].to_broadcast([P, NT, K]),
                                    ALU.subtract).then_inc(soft_in, 1)
            for t in range(NT):
                last = nc.vector.max_index(topi[:, t, :], top[:, t, :], logit[:, t, :])
            link(last)
            link(nc.vector.tensor_copy(topf[:, :, :], topi[:, :, 0:K]))
            iota_e = const(ca, CA, "iota_e")
            link(nc.vector.tensor_tensor(
                hot[:, :, :, :].rearrange("p t k e -> p (t k) e"),
                iota_e.rearrange("p (o e) -> p o e", o=1).to_broadcast([P, NT * K, E]),
                topf[:, :, :].rearrange("p t (k o) -> p (t k) o", o=1).to_broadcast([P, NT * K, E]), ALU.is_equal))
            link(nc.vector.memset(ones[:, :], 1.0))
            nc.vector.tensor_reduce(sel[:, :, :], hot[:, :, :, :].rearrange("p t k e -> p t e k"), axis=AX.X,
                                    op=ALU.add).then_inc(sel_ready, 1)
            dve.wait_ge(soft_out, 1)
            link(nc.vector.tensor_reduce(wsum[:, :], weight[:, :, :], axis=AX.X, op=ALU.add))
            link(nc.vector.reciprocal(wsum[:, :], wsum[:, :]))
            nc.vector.tensor_tensor(weight[:, :, :], weight[:, :, :],
                                    wsum[:, :].rearrange("p (t o) -> p t o", o=1).to_broadcast([P, NT, K]), ALU.mult)

            quad = const(cc, CC, "quad").rearrange("p (o h k) -> p o h k", o=1, k=1).to_broadcast([P, HKV, G, NBLK])
            for bd, rep, n_rep in ((bd_s, rep_s, HKV), (bd_g, rep_g, 2 * HKV)):
                dve.wait_ge(rep_kept, n_rep)
                for b in range(NB):
                    last = nc.vector.tensor_tensor(bd[:, b, :, :, :],
                                                   rep[:, :, b, 0:NBLK].rearrange("p g (o k) -> p g o k", o=1).to_broadcast([P, HKV, G, NBLK]),
                                                   quad, ALU.mult)
                last.then_inc(diagonals_ready, 1)
            pmask = const(cc, CC, "pair")
            dve.wait_ge(zeros_ready, 2)
            for g in range(HKV):
                dve.wait_ge(wv_done, g + 1)
                rep = bank[(7, 1, 2, 3)[g]][:, 0:NB * NKEY].rearrange("p (b k) -> p b k", b=NB)
                for b in range(NB):
                    for m in range(2):
                        n = 2 * g + m
                        col = 2 * (n % 4) * NBLK
                        nc.vector.tensor_tensor(
                            vb[:, b, n, col:col + 2 * NBLK].rearrange("p (h k) -> p h k", h=2),
                            rep[:, b, 0:NBLK].rearrange("p (o k) -> p o k", o=1).to_broadcast([P, 2, NBLK]),
                            pmask.rearrange("p (h o) -> p h o", o=1).to_broadcast([P, 2, NBLK]), ALU.mult)
                last = nc.vector.tensor_reduce(vsum[:, :, g], rep[:, :, NBLK:NKEY], axis=AX.X, op=ALU.add)
            link(last)
            for b in range(NB):
                for g in range(HKV):
                    n = 2 * g if g >= 2 else 8 + 2 * g
                    last = nc.vector.tensor_copy(vb[:, b, n:n + 2, HALF:HALF + 1], vsum[:, b, g:g + 1].rearrange("p (o n) -> p o n", o=1).to_broadcast([P, 2, 1]))
            last.then_inc(diagonals_ready, 1)

            dve.wait_ge(ranked, 1)
            link(nc.vector.tensor_copy(tot[:, :, :], bank[0][:, 0:NT * E].rearrange("p (t e) -> p e t", t=NT)))
            link(nc.vector.tensor_tensor_scan(cum[:, :, :].rearrange("p e t -> p (e t)"), const(ca, CA, "carry"),
                                              tot[:, :, :].rearrange("p e t -> p (e t)"), 0.0, ALU.mult, ALU.add))
            link(nc.vector.tensor_scalar(cnt[:, :], cum[:, :, NT - 1], float(P - 1), None, ALU.add))
            link(nc.vector.tensor_copy(nt_i[:, :], cnt[:, :]))
            link(nc.vector.tensor_scalar(nt_i[:, :], nt_i[:, :], 7, None, ALU.logical_shift_right))
            link(nc.vector.tensor_copy(nt_f[:, :], nt_i[:, :]))
            link(nc.vector.tensor_tensor_scan(ends[:, :], ones[:, 0:E], nt_f[:, :], 0.0, ALU.mult, ALU.add))
            link(nc.vector.tensor_tensor(nt_f[:, :], ends[:, :], nt_f[:, :], ALU.subtract))
            link(nc.vector.tensor_tensor(cum[:, :, :], cum[:, :, :], tot[:, :, :], ALU.subtract))
            link(nc.vector.tensor_scalar(nt_f[:, :], nt_f[:, :], float(P), None, ALU.mult))
            link(nc.vector.tensor_tensor(cum[:, :, :], cum[:, :, :], nt_f[:, :].rearrange("p (e o) -> p e o", o=1).to_broadcast([P, E, NT]), ALU.add))
            link(nc.vector.tensor_tensor(sel[:, :, :], cum[:, :, :].rearrange("p e t -> p t e"),
                                         bank[4][:, NT * E:2 * NT * E].rearrange("p (t e) -> p t e", t=NT), ALU.add))
            link(nc.vector.tensor_tensor(hot[:, :, :, :], hot[:, :, :, :],
                                         sel[:, :, :].rearrange("p t (o e) -> p t o e", o=1).to_broadcast([P, NT, K, E]), ALU.mult))
            link(nc.vector.tensor_reduce(pos[:, :], hot[:, :, :, :].rearrange("p t k e -> p (t k) e"), axis=AX.X, op=ALU.add))
            link(nc.vector.tensor_copy(pos_i[:, :], pos[:, :]))
            link(nc.vector.tensor_scalar(topi[:, :, :].rearrange("p t k -> p (t k)")[:, 0:NT * K].bitcast(I32), pos_i[:, :], 7, None,
                                         ALU.logical_shift_right))
            link(nc.vector.tensor_scalar(pos_i[:, :], pos_i[:, :], P - 1, None, ALU.bitwise_and))
            nc.vector.tensor_copy(jf[:, :], topi[:, :, :].rearrange("p t k -> p (t k)")[:, 0:NT * K].bitcast(I32))
            link(nc.vector.tensor_copy(rf[:, :], pos_i[:, :]))

            column = const(ca, CA, "column")
            iota_p = const(ca, CA, "iota_p")
            iota_j = const(ca, CA, "iota_j")
            hide_l = const(cc, CC, "hide_l")

            def rope_q(raw_bank, u, t):
                raw = raw_bank[:, :].rearrange("p (g h d) -> p g h d", g=H, h=2)
                t2 = q2[:, :].rearrange("p (g h d) -> p g h d", g=H, h=2)
                co = cos[:, ds(t * RH, RH)].rearrange("p (o d) -> p o d", o=1).to_broadcast([P, 2 * H, RH])
                nc.vector.tensor_tensor(q1[u][:, :].rearrange("p (g d) -> p g d", d=RH), raw_bank[:, :].rearrange("p (g d) -> p g d", d=RH), co, ALU.mult)
                for half in range(2):
                    sn = sin[:, ds(t * DS + half * RH, RH)].rearrange("p (o d) -> p o d", o=1).to_broadcast([P, H, RH])
                    last = nc.vector.tensor_tensor(t2[:, :, half, :], raw[:, :, 1 - half, :], sn, ALU.mult)
                return last

            def rope_sum(u, done):
                nc.vector.tensor_tensor(q1[u][:, :], q1[u][:, :], q2[:, :], ALU.add).then_inc(done, 1)

            def over_keys(v, n=H, k=NBLK):
                return v.rearrange("p (h o) -> p h o", o=1).to_broadcast([P, n, k])

            for u in range(NB):
                dve.wait_ge(l_q, u + 1)
                if u:
                    dve.wait_ge(l_rope, u)
                nc.vector.tensor_copy(pr[u][:, HK:HK + 1], even[:, REMOTE:TB])
                link(rope_q(bank[(3, 2)[u]], u, REMOTE))
                rope_sum(u, l_rope)

            def l_scores(n):
                q = n % 2
                dve.wait_ge(l_s, n + 1)
                if n >= 2:
                    dve.wait_ge(l_ex, n - 1)
                for h in range(G):
                    last = nc.vector.tensor_tensor(l2[q][:, h, :], bank[L_BANKS[h]][:, 0:NKEY], hide_l, ALU.add)
                last.then_inc(l_read, 1)
                dve.wait_ge(l_read, n + 1)
                link(nc.vector.tensor_reduce(lmax[q][:, :], l2[q][:, :, :], axis=AX.X, op=ALU.max))
                nc.vector.tensor_scalar(lneg[q][:, :], lmax[q][:, :], -1.0, None, ALU.mult).then_inc(l_max, 1)

            def l_probabilities(n):
                q, u, g = n % 2, n // HKV, n % HKV
                dve.wait_ge(l_ex, n + 1)
                link(nc.vector.reciprocal(lrec[n % 4][:, :], lsum[q][:, :]))
                nc.vector.tensor_tensor(pr[u][:, g * G * NBLK:(g + 1) * G * NBLK].rearrange("p (h k) -> p h k", h=G),
                                        lex[q][:, :, 0:NBLK], over_keys(lrec[n % 4][:, :], G, NBLK), ALU.mult).then_inc(l_p, 1)

            for h in range(2):
                dve.wait_ge(xn_stored[h], GROUPS // 2 * DMA)

            def l_values(n):
                q, u, g = n % 2, n // HKV, n % HKV
                dve.wait_ge(l_pv, n + 1)
                nc.vector.tensor_tensor(osb[u][:, g * G * DV:(g + 1) * G * DV].rearrange("p (h d) -> p h d", h=G),
                                        bank[7][:, 0:D].rearrange("p (h d) -> p h d", h=G),
                                        over_keys(lrec[n % 4][:, :], G, DV), ALU.mult).then_inc(l_osb, 1)

            def onehot_rows(n):
                if n >= 2:
                    dve.wait_ge(pair_used, n - 1)
                cols = slice(n * CHUNK, (n + 1) * CHUNK)
                j = onehot_j[n % 2]

                def each(v, width, o="p (c o) -> p c o"):
                    return v.rearrange(o, o=1).to_broadcast([P, CHUNK, width])

                link(nc.vector.tensor_tensor(j[:, :, 0, :], each(iota_j, NS, "p (o r) -> p o r"), each(jf[:, cols], NS), ALU.is_equal))
                nc.vector.tensor_tensor(onehot_p[n % 2][:, :, :], each(iota_p, P, "p (o r) -> p o r"), each(rf[:, cols], P), ALU.is_equal)
                link(nc.vector.tensor_scalar(j[:, :, 1, :], j[:, :, 0, :], const(ca, CA, "row"), None, ALU.mult))
                nc.vector.tensor_tensor(j[:, :, 0, :], j[:, :, 0, :], each(column[:, cols], NS), ALU.mult).then_inc(pair_ready, 1)

            onehot_rows(0)
            for n in range(UNITS):
                l_scores(n)
                if n >= 1:
                    l_probabilities(n - 1)
                    l_values(n - 1)
                if n + 1 < UNITS:
                    onehot_rows(n + 1)

            link(nc.vector.tensor_tensor(cmp_j[:, :, :], ends[0:1, :].rearrange("p (o e) -> p o e", o=1).to_broadcast([1, NS, E]),
                                         iota_j[0:1, :].rearrange("p (j o) -> p j o", o=1).to_broadcast([1, NS, E]), ALU.is_le))
            link(nc.vector.tensor_reduce(te_f[:, :], cmp_j[:, :, :], axis=AX.X, op=ALU.add))
            link(nc.vector.tensor_scalar(te_f[:, :], te_f[:, :], float(E - 1), None, ALU.min))
            link(nc.vector.tensor_copy(te_i[:, :], te_f[:, :]))
            l_probabilities(UNITS - 1)
            l_values(UNITS - 1)
            dve.wait_ge(inverse_done, 1)
            link(nc.vector.scalar_tensor_tensor(pad_f[:, :], bank[0][:, NS:2 * NS], 0.0, const(ca, CA, "trash"), ALU.is_equal, ALU.mult))
            link(nc.vector.scalar_tensor_tensor(pad_f[:, :], bank[0][:, NS:2 * NS], -1.0, pad_f[:, :], ALU.add, ALU.add))
            link(nc.vector.tensor_scalar(dest_f[:, :], bank[0][:, 0:NS], float(P), None, ALU.mult))
            link(nc.vector.tensor_tensor(dest_f[:, :], dest_f[:, :], pad_f[:, :], ALU.add))
            link(nc.vector.tensor_copy(dest_i[:, :], dest_f[:, :]))
            link(nc.vector.tensor_scalar(dest_f[:, :], dest_f[:, :], const(ca, CA, "pad_row"), None, ALU.min))
            link(nc.vector.tensor_copy(tok_i[:, :], dest_f[:, :]))
            link(nc.vector.tensor_scalar(tok_hi[:, :], tok_i[:, :], 9, 7, ALU.logical_shift_right, ALU.logical_shift_left))
            link(nc.vector.tensor_scalar(tok_lo[:, :], tok_i[:, :], P - 1, None, ALU.bitwise_and))
            nc.vector.tensor_tensor(tok_i[:, :], tok_hi[:, :], tok_lo[:, :], ALU.bitwise_or).then_inc(lists_ready, 1)

            def l_attended(u):
                dve.wait_ge(lx_in, NB * DMA)
                dve.wait_ge(l_o, u + 1)
                nc.vector.tensor_tensor(xr[u][:, :], bank[L_OUT[u]][:, 0:D], xr[u][:, :], ALU.add).then_inc(c_out[u], 1)

            def heads_of(v):
                return v[:, 0:HK].rearrange("p (h k) -> p h k", h=H)

            def rope(u, t):
                dve.wait_ge(c_q[u], t.count(1))
                if not t.first:
                    dve.wait_ge(c_qt[u], t.count(0))
                if u or not t.first:
                    dve.wait_ge(c_rope[1 - u], t.count(u))
                rope_q(bank[2 + u], u, t.number).then_inc(c_rot[u], 1)
                dve.wait_ge(c_rot[u], t.count(1))
                rope_sum(u, c_rope[u])

            def shifted(u, t):
                dve.wait_ge(c_s[u], t.count(1))
                if not t.first:
                    dve.wait_ge(c_pt[u], t.count(0))
                nc.vector.scalar_tensor_tensor(
                    heads_of(pr[u]), bank[6 + u][:, 0:HK].rearrange("p (h k) -> p h k", h=H), any_key[:, ds(t.number, 1)],
                    hide[:, ds(t.number * NBLK, NBLK)].rearrange("p (o k) -> p o k", o=1).to_broadcast([P, H, NBLK]), ALU.mult, ALU.add).then_inc(c_masked[u], 1)
                dve.wait_ge(c_masked[u], t.count(1))
                nc.vector.tensor_reduce(smax[u][:, :], heads_of(pr[u]), axis=AX.X, op=ALU.max).then_inc(c_max[u], 1)
                nc.vector.tensor_copy(pr[u][:, HK:HK + 1], even[:, ds(t.number, 1)])
                dve.wait_ge(c_max[u], t.count(1))
                nc.vector.tensor_tensor(heads_of(pr[u]), heads_of(pr[u]), over_keys(smax[u][:, :]), ALU.subtract).then_inc(c_d[u], 1)

            def row_sum(u, t):
                dve.wait_ge(c_ex[u], t.count(1))
                nc.vector.tensor_reduce(ssum[:, u, :], heads_of(pr[u]), axis=AX.X, op=ALU.add).then_inc(c_sum, 1)

            def probabilities(t):
                dve.wait_ge(c_sum, 2 * t.number + 2)
                if t.first:
                    nc.vector.tensor_scalar(ssum[:, :, :], ssum[:, :, :], more[:, 0:1], None, ALU.add).then_inc(c_all, 1)
                    dve.wait_ge(c_all, 1)
                nc.vector.reciprocal(srec[:, :, :], ssum[:, :, :]).then_inc(c_rec, 1)
                dve.wait_ge(c_rec, t.count(1))
                for u in range(NB):
                    nc.vector.tensor_tensor(heads_of(pr[u]), heads_of(pr[u]), over_keys(srec[:, u, :]), ALU.mult).then_inc(c_p[u], 1)

            def attended(u, t):
                dve.wait_ge(c_o[u], t.count(1))
                dve.wait_ge(xr_in[u], (t.number + 1) * DMA)
                nc.vector.tensor_tensor(xr[u][:, :], bank[4 + u][:, 0:D], xr[u][:, :], ALU.add).then_inc(c_out[u], 1)

            def rows_in(t):
                if not t.first_there():
                    dve.wait_ge(gathered[t.place], t.dmas())
                nc.vector.tensor_scalar(idx_in[t.place][:, :], tok_i[:, ds(t.number, 1)], 0.0, None, ALU.add).then_inc(in_idx, 1)

            def attention(t):
                if t.off == REMOTE - 1:
                    for u in range(NB):
                        dve.wait_ge(c_rope[u], REMOTE)
                    for r in range(4):
                        rows_in(Tile(0, r))
                for u in range(NB):
                    if t.more(1).exists:
                        rope(u, t.more(1))
                    shifted(u, t)
                row_sum(0, t)
                if not t.first:
                    for u in range(NB):
                        attended(u, t.more(-1))
                row_sum(1, t)
                probabilities(t)

            for u in range(NB):
                l_attended(u)
                rope(u, Pair(0, 0))
            pairs(dve, attention)
            for u in range(NB):
                attended(u, Pair(0, REMOTE - 1))

            def step(j):
                t = j + 2
                if t.exists:
                    dve.wait_ge(xh_ready, t.done)
                    nc.vector.tensor_tensor(xl[t.par][:, :, :], bank[t.par][:, 0:D].rearrange("p (c n) -> p c n", c=DC),
                                            xh[t.par][:, :, :].bitcast(F32), ALU.subtract).then_inc(xl_ready, 1)
                t = j + 6
                if t.exists:
                    rows_in(t)
                t = j + 1
                if t.exists:
                    dve.wait_ge(sg_ready, t.done)
                    nc.vector.tensor_tensor(av[t.par][:, :], bank[2 + t.par][:, I:2 * I], sg[t.par][:, :], ALU.mult).then_inc(av_ready, 1)
                t = j
                if t.exists:
                    dve.wait_ge(ah_ready, t.done)
                    nc.vector.tensor_tensor(al[t.par][:, :, :], bank[4 + t.par][0:IH, 0:2 * P].rearrange("p (c n) -> p c n", c=2),
                                            ah[t.par][:, :, :].bitcast(F32), ALU.subtract).then_inc(al_ready, 1)
                t = j + -1
                if t.exists:
                    if not t.first_there():
                        dve.wait_ge(scattered[t.place], t.dmas())
                    nc.vector.tensor_scalar(idx_out[t.place][:, :], dest_i[:, ds(t.number, 1)], 0.0, None, ALU.add).then_inc(out_idx, 1)

            steps(dve, step, (NS - 7) // ROUND)

            w_all = weight[:, :, :].rearrange("p t k -> p (t k)")
            dve.wait_ge(part_in, DMA)
            with dve.Fori(0, NT // 4) as i:
                for s0 in (0, 2):
                    for k in range(K):
                        for s in (s0, s0 + 1):
                            z = 4 * i + s
                            if k == 0:
                                dve.wait_ge(yv_in[s], (i + 1) * DMA)
                            else:
                                dve.wait_ge(t_link[s % 2], (2 * i + s // 2) * (K - 1) + k)
                            o = total[:, :, :].rearrange("p t d -> p (t d)")[:, ds(z * D, D)]
                            acc = part[:, :, :].rearrange("p t d -> p (t d)")[:, ds(z * D, D)] if k == 0 else o
                            ins = nc.vector.scalar_tensor_tensor(o, yv[s][:, k, :], w_all[:, ds(z * K + k, 1)], acc, ALU.mult, ALU.add)
                            ins.then_inc(t_link[s % 2] if k < K - 1 else total_ready[s], 1)

        @block.tensor
        def _(pe):
            def mm(o, lhsT, rhs, start, stop):
                return nc.tensor.matmul(o, lhsT, rhs, start=start, stop=stop)

            pe.wait_ge(const_in, 4 * DMA)
            for c in range(DC):
                last = nc.tensor.transpose(bank[6][:, c * E:(c + 1) * E], rw[:, c * P:(c + 1) * P], ident[0:E, 0:E])
            last.then_inc(rw_t, 1)

            def turn(t):
                if t >= 3:
                    pe.wait_ge(xT_ready, t - 2)
                for b in range(NB):
                    pe.wait_ge(xn_ready, NB * t + b + 1)
                    for c in range(DC):
                        at = b * D + c * P
                        last = nc.tensor.transpose(bank[t % 3][:, at:at + P], x_all[:, t * NB + b, c * P:(c + 1) * P], ident)
                last.then_inc(xn_turned, 1)

            def project(t):
                if t == 0:
                    pe.wait_ge(rwT_ready, 1)
                pe.wait_ge(xT_ready, t + 1)
                if t >= 4:
                    pe.wait_ge(rope_done, t - 3)
                for b in range(NB):
                    for c in range(DC):
                        last = mm(bank[3 + t % 4][:, b * (KD + E):(b + 1) * (KD + E)], xT[t // 2 % 2][:, t % 2 * NB + b, c, :], wkr[:, c, :], c == 0, c == DC - 1)
                last.then_inc(k_raw, 1)

            def block_means(t):
                pe.wait_ge(rope_done, t + 1)
                for b in range(NB):
                    at = b * 2 * TB + 2 * t
                    last = mm(bank[7][:, at:at + 2], rope1[t // 2 % 2][:, t % 2, b, :], pool2, True, True)
                last.then_inc(pooled, 1)

            turn(0)
            turn(1)
            for t in range(TB):
                if t + 2 < TB:
                    turn(t + 2)
                project(t)
                if t >= 1:
                    block_means(t - 1)
            block_means(TB - 1)
            for b in range(NB):
                last = nc.tensor.transpose(bank[7][:, (1 + b) * P:(2 + b) * P], rope1[1][:, 1, b, :], ident)
            last.then_inc(keys_turned, 1)

            pe.wait_ge(q_in, 3 * DMA)
            pe.wait_ge(xT_ready, TB)
            pe.wait_ge(rope_done, TB)
            for g in range(HKV):
                for c in range(DC):
                    at = (g % 2) * D + c * P
                    last = nc.tensor.transpose(bank[2 + g // 2][:, at:at + P], wqs[:, c, g * P:(g + 1) * P], ident)
            last.then_inc(wqT_done, 1)
            pe.wait_ge(kv_in, 5 * DMA)
            pe.wait_ge(wrep_ready, 1)
            pe.wait_ge(keys_kept, 1)
            copies = const(cc, CC, "copies")
            for n in range(2 * HKV):
                g, b = n % HKV, bank[(5, 6, 2, 3)[n % 4]]
                if n == 2:
                    pe.wait_ge(wqT_ready, 1)
                if n >= 4:
                    pe.wait_ge(rep_kept, n - 3)
                o = b[:, 0:NB * NKEY]
                if n < HKV:
                    for c in range(DC):
                        last = mm(o, wk_rep[:, c, g, :, :].rearrange("p h d -> p (h d)"), x_keys[:, c, :, :].rearrange("p b k -> p (b k)"), c == 0, c == DC - 1)
                else:
                    last = mm(o, copies[:, g * P:(g + 1) * P], kgeo_t[:, :, :].rearrange("p b k -> p (b k)"), True, True)
                last.then_inc(rep_done, 1)
            for g in range(HKV):
                if g >= 2:
                    pe.wait_ge(rep_kept, 5 + g)
                for c in range(DC):
                    last = mm(bank[(7, 1, 2, 3)[g]][:, 0:NB * NKEY], wv_rep[:, c, g, :, :].rearrange("p h d -> p (h d)"),
                              x_keys[:, c, :, :].rearrange("p b k -> p (b k)"), c == 0, c == DC - 1)
                last.then_inc(wv_done, 1)
            pe.wait_ge(sel_ready, 1)
            sel_v = sel[:, :, :].rearrange("p t e -> p (t e)")
            mm(bank[4][:, NT * E:2 * NT * E], below, sel_v, True, True)
            mm(bank[0][:, 0:NT * E], ones[:, :], sel_v, True, True).then_inc(ranked, 1)
            pe.wait_ge(diagonals_ready, 1)
            pe.wait_ge(rep_kept, 2 * HKV)
            for b in range(NB):
                for c in range(DC):
                    for g in range(HKV):
                        at = c * HK + g * G * NBLK
                        last = mm(bank[5 + b][:, at:at + G * NBLK], wqT[:, g, c * P:(c + 1) * P],
                                  bd_s[:, b, g, :, :].rearrange("p h k -> p (h k)"), True, True)
                last.then_inc(set_done, 1)

            pe.wait_ge(diagonals_ready, 3)
            x_last = [xT[1][:, 2 + u, :, :] for u in range(NB)]
            for u in range(NB):
                for c in range(DC):
                    last = mm(bank[(3, 2)[u]][:, :], x_last[u][:, c, :], wqg[:, c, :], c == 0, c == DC - 1)
                last.then_inc(l_q, 1)
            for b in range(NB):
                for c in range(DC):
                    last = mm(bank[1][:, b * D:(b + 1) * D], x_keys[:, c, b, NBLK:NKEY], wv_s[:, c, :], c == 0, c == DC - 1)
            last.then_inc(set_done, 1)
            pe.wait_ge(set_kept, NB)
            for u in range(NB):
                for g in range(HKV):
                    for c in range(DC):
                        last = mm(bank[6 + u][:, g * P:(g + 1) * P], wqs[:, c, g * P:(g + 1) * P], x_last[u][:, c, :], c == 0, c == DC - 1)
                last.then_inc(l_qs, 1)

            def turn_queries(o, u):
                for g in range(HKV):
                    last = nc.tensor.transpose(o[:, g * P:(g + 1) * P], q1[u][:, g * P:(g + 1) * P], ident)
                return last

            for u in range(NB):
                pe.wait_ge(l_rope, u + 1)
                turn_queries(bank[(5, 3)[u]], u).then_inc(l_qt, 1)

            def l_score(n):
                u, g = n // HKV, n % HKV
                if n == 0:
                    pe.wait_ge(l_qT, NB)
                    pe.wait_ge(l_qsT, NB)
                    pe.wait_ge(set_kept, NB + 1)
                else:
                    pe.wait_ge(l_read, n)
                for h in range(G):
                    o = bank[L_BANKS[h]][:, 0:NKEY]
                    own = slice(h * DS, (h + 1) * DS)
                    mm(o, qrT[u][own, g, :], rep_g[own, g, u, :], True, False)
                    last = mm(o, qsT[u][own, g, :], rep_s[own, g, u, :], False, True)
                last.then_inc(l_s, 1)

            def invert(n):
                pe.wait_ge(pair_ready, n + 1)
                for m in range(CHUNK):
                    last = mm(bank[0][:, 0:2 * NS], onehot_p[n % 2][:, m, :], onehot_j[n % 2][:, m, :, :].rearrange("p d j -> p (d j)"), n == 0 and m == 0, n == UNITS - 1 and m == CHUNK - 1)
                last.then_inc(pair_used if n < UNITS - 1 else inverse_done, 1)

            def l_turn(n):
                pe.wait_ge(l_ex, n + 1)
                if n >= 1:
                    pe.wait_ge(l_pT, n)
                for h in range(G):
                    last = nc.tensor.transpose(bank[6][:, h * P:(h + 1) * P], lex[n % 2][:, h, NBLK:NKEY], ident)
                last.then_inc(l_t, 1)

            def l_value(n):
                u, g = n // HKV, n % HKV
                pe.wait_ge(l_pT, n + 1)
                if n >= 1:
                    pe.wait_ge(l_osb, n)
                for h in range(G):
                    last = mm(bank[7][:, h * DV:(h + 1) * DV], lpT[n % 2][:, h, :], vloc[:, u, g * DV:(g + 1) * DV], True, True)
                last.then_inc(l_pv, 1)

            def fold_values(n):
                b, third = n // HKV, n % HKV
                if b and third == 0:
                    pe.wait_ge(set_kept, NB + 2)
                for m in range(4 * third, 4 * third + 4):
                    if m < 4:
                        last = mm(bank[4][0:HALF, 0:D], vb[:, b, m, 0:HALF], wo_s[:, m, :], m == 0, m == 3)
                    else:
                        last = mm(bank[4][0:HALF + 1, D:2 * D], vb[:, b, m, :], wo_s[:, m % 8, :], m == 4, m == 11)
                if third == 2:
                    last.then_inc(set_done, 1)

            def turn_values(u):
                pe.wait_ge(l_osb, HKV * (u + 1))
                for n in range(8):
                    at = n % 4 * P
                    last = nc.tensor.transpose(bank[L_TURNED[u][n // 4]][:, at:at + P], osb[u][:, n * P:(n + 1) * P], ident)
                last.then_inc(l_ot, 1)

            def turn_probabilities(u):
                pe.wait_ge(l_p, HKV * (u + 1))
                if u:
                    pe.wait_ge(l_prT, u)
                nc.tensor.transpose(bank[4][0:HALF, 0:P], pr[u][:, 0:HALF], ident)
                nc.tensor.transpose(bank[4][0:HALF + 1, P:D], pr[u][:, HALF:HK + 1], ident).then_inc(l_pt, 1)

            def l_attend(u):
                o = bank[L_OUT[u]][:, 0:D]
                pe.wait_ge(l_oT, u + 1)
                for n in range(8):
                    mm(o, oT[u][:, n, :], wo_s[:, n, :], n == 0, False)
                pe.wait_ge(l_prT, u + 1)
                mm(o, prT[u][0:HALF, 0, :], vw[0:HALF, u, 0, :], False, False)
                mm(o, prT[u][:, 1, :], vw[:, u, 1, :], False, True).then_inc(l_o, 1)

            l_score(0)
            invert(0)
            for n in range(UNITS):
                if n + 1 < UNITS:
                    l_score(n + 1)
                l_turn(n)
                if n % HKV < HKV - 1:
                    fold_values(n)
                if n + 1 < UNITS:
                    invert(n + 1)
                else:
                    pe.wait_ge(l_read, UNITS)
                    turn_values(0)
                l_value(n)
            pe.wait_ge(set_kept, 2 * NB + 1)
            turn_probabilities(0)
            l_attend(0)
            pe.wait_ge(l_pT, UNITS)
            turn_values(1)
            turn_probabilities(1)

            def x_turn(u, t):
                pe.wait_ge(xc_in[u], (t.number + 1) * DMA)
                for c in range(DC):
                    last = nc.tensor.transpose(bank[u][:, c * P:(c + 1) * P], xc[u][:, c * P:(c + 1) * P], ident)
                last.then_inc(c_xt[u], 1)

            def q_project(u, t):
                pe.wait_ge(c_xT[u], t.count(1))
                for c in range(DC):
                    last = mm(bank[2 + u][:, :], xcT[u][t.par][:, c, :], wqg[:, c, :], c == 0, c == DC - 1)
                last.then_inc(c_q[u], 1)

            def q_turn(u, t):
                pe.wait_ge(c_rope[u], t.count(1))
                if not t.first:
                    pe.wait_ge(c_out[u], t.count(0))
                turn_queries(bank[4 + u], u).then_inc(c_qt[u], 1)

            def score(u, t):
                pe.wait_ge(c_qT[u], t.count(1))
                if not t.first:
                    pe.wait_ge(c_d[u], t.count(0))
                for c in range(DC):
                    mm(bank[6 + u][:, 0:HK], xcT[u][t.par][:, c, :], asem[:, u, c, :], c == 0, False)
                for g in range(HKV):
                    last = mm(bank[6 + u][:, g * G * NBLK:(g + 1) * G * NBLK], qrT[u][:, g, :], bd_g[:, u, g, :, :].rearrange("p h k -> p (h k)"),
                              False, g == HKV - 1)
                last.then_inc(c_s[u], 1)

            def p_turn(u, t):
                pe.wait_ge(c_p[u], t.count(1))
                if t.more(2).exists:
                    pe.wait_ge(c_xT[u], t.count(3))
                nc.tensor.transpose(bank[u][0:HALF, D:D + P], pr[u][:, 0:HALF], ident)
                nc.tensor.transpose(bank[u][0:HALF + 1, D + P:2 * D], pr[u][:, HALF:HK + 1], ident).then_inc(c_pt[u], 1)

            def attend(u, t):
                pe.wait_ge(c_pT[u], t.count(1))
                o = bank[4 + u][:, 0:D]
                mm(o, prT[u][0:HALF, 0, :], vw[0:HALF, u, 0, :], True, False)
                mm(o, prT[u][:, 1, :], vw[:, u, 1, :], False, True).then_inc(c_o[u], 1)

            def attention_pe(t):
                for u in range(NB):
                    q_turn(u, t)
                for u in range(NB):
                    if t.more(1).exists:
                        q_project(u, t.more(1))
                    score(u, t)
                    if u == 0 and not t.first:
                        for v in range(NB):
                            p_turn(v, t.more(-1))
                if not t.first:
                    for u in range(NB):
                        attend(u, t.more(-1))
                if t.more(2).exists:
                    for u in range(NB):
                        x_turn(u, t.more(2))

            pe.wait_ge(lists_ready, 1)
            pe.wait_ge(l_oT, 1)
            for u in range(NB):
                x_turn(u, Pair(0, 0))
            q_project(0, Pair(0, 0))
            l_attend(1)
            q_project(1, Pair(0, 0))
            for u in range(NB):
                x_turn(u, Pair(0, 1))
            for u in range(NB):
                pe.wait_ge(c_out[u], 1)
            pairs(pe, attention_pe)
            for u in range(NB):
                p_turn(u, Pair(0, REMOTE - 1))
            for u in range(NB):
                attend(u, Pair(0, REMOTE - 1))

            pe.wait_ge(w_lo, E)

            def three(o, hi, lo, w_hi_, w_lo_, e, width):
                for c in range(2):
                    cols = ds((e * 2 + c) * width, width)
                    mm(o, hi[:, c, :], w_hi_[:, cols], c == 0, False)
                    mm(o, hi[:, c, :], w_lo_[:, cols], False, False)
                    last = mm(o, lo[:, c, :], w_hi_[:, cols], False, c == 1)
                return last

            known = {}

            def expert(t):
                if t.counts is None or t.r < 2 or t.r not in known:
                    e = pe.value_load(te_i[0:1, ds(t.number, 1)], min_val=0, max_val=E - 1)
                    if t.counts is None:
                        return e
                    known[t.r] = e
                return known[t.r]

            def step(j):
                t = j + 2
                if t.exists:
                    pe.wait_ge(gathered[t.place], t.dmas(1))
                    for c in range(DC):
                        last = nc.tensor.transpose(bank[t.par][:, c * P:(c + 1) * P], xg[t.place][:, c * P:(c + 1) * P], ident)
                    last.then_inc(x_turned, 1)
                t = j + 1
                if t.exists:
                    e = expert(t)
                    pe.wait_ge(xl_ready, t.done)
                    three(bank[2 + t.par][:, 0:2 * I], xh[t.par], xl[t.par], wgu_h, wgu_l, e, 2 * I).then_inc(gu_done, 1)
                t = j
                if t.counts is None and t.r == 0:
                    for u in range(NB):
                        pe.wait_ge(c_out[u], TB)
                if t.exists:
                    pe.wait_ge(av_ready, t.done)
                    for c in range(2):
                        last = nc.tensor.transpose(bank[4 + t.par][0:IH, c * P:(c + 1) * P], av[t.par][:, c * IH:(c + 1) * IH], ident)
                    last.then_inc(av_turned, 1)
                t = j + -1
                if t.exists:
                    e = expert(t)
                    pe.wait_ge(al_ready, t.done)
                    three(bank[6 + t.par][:, 0:D], ah[t.par], al[t.par], wdn_h, wdn_l, e, D).then_inc(y_done, 1)

            steps(pe, step, (NS - 3) // ROUND)


def constants():
    import numpy as np

    f = np.float32
    p = np.arange(P)
    k, a, c = (np.zeros((P, n), f) for n in (NCK, NCA, NCC))

    def put(m, table, name, v):
        at, n = table[name]
        m[:, at:at + n] = np.asarray(v, f).reshape(P, n)

    inv = (1.0 / np.power(f(10000.0), np.arange(0, DS, 2, dtype=f) / f(DS))).astype(f)
    ang = (np.arange(T, dtype=f)[:, None] * inv).astype(f)
    cos, sin = np.cos(ang).astype(f), np.sin(ang).astype(f)
    tiles = lambda v: v.reshape(TB, P, -1).transpose(1, 0, 2)
    pos = np.arange(TB)[:, None] * P + p[None, :]
    see = (np.arange(NBLK) * MB + MB - 1)[None, None, :] <= pos[:, :, None]
    none = pos.T < MB - 1
    put(k, CK, "ident", np.eye(P))
    put(k, CK, "cos", tiles(cos))
    put(k, CK, "sin", tiles(np.concatenate([-sin, sin], 1)))
    put(k, CK, "hide", np.where(see, 0.0, NEG).transpose(1, 0, 2))
    put(k, CK, "any", ~none)
    put(k, CK, "more", none * LW)
    put(k, CK, "even", none / f(NKEY))
    put(a, CA, "below", p[:, None] < p[None, :])
    put(a, CA, "pool", np.stack([p < MB, p >= MB], 1) / f(MB))
    put(a, CA, "iota_e", np.tile(np.arange(E), (P, 1)))
    put(a, CA, "iota_j", np.tile(np.arange(NS), (P, 1)))
    put(a, CA, "iota_p", np.tile(p, (P, 1)))
    put(a, CA, "column", np.tile(np.arange(NT * K), (P, 1)))
    put(a, CA, "row", p + 1)
    put(a, CA, "trash", NROW + 1 + np.arange(NS)[None, :] * P + p[:, None])
    put(a, CA, "pad_row", N * K + p)
    put(a, CA, "carry", np.tile(np.arange(NT) > 0, (P, E)))
    put(c, CC, "heads", (p[:, None] // DS == np.arange(H)[None, :] % G) * f(SCALE))
    put(c, CC, "pair", p[:, None] // DV == np.arange(2)[None, :])
    put(c, CC, "quad", p[:, None] // DS == np.arange(G)[None, :])
    put(c, CC, "hide_l", np.concatenate([np.zeros((P, NBLK)), np.where(p[None, :] <= p[:, None], 0.0, NEG)], 1))
    put(c, CC, "copies", np.stack([p[:, None] == g * DS + p[None, :] % DS for g in range(HKV)], 1))
    return k, a, c


INPUTS = ["L0_attn_x", "L0_attn_Wq_sem", "L0_attn_Wk_sem", "L0_attn_Wq_geo", "L0_attn_Wk_geo", "L0_attn_Wv", "L0_attn_Wo",
          "L0_attn_logit_scale", "L0_ffn_router_w", "L0_ffn_expert_bias", "L0_ffn_gate_proj", "L0_ffn_up_proj", "L0_ffn_down_proj"]


def kernel(**inputs):
    import numpy as np
    import concourse.bacc as bacc
    from concourse.bass_utils import run_bass_kernel_spmd

    nc = bacc.Bacc("TRN2", target_bir_lowering=False, num_devices=1, dynamic_dma_scratch_size=8192)
    arrays = {name: np.ascontiguousarray(inputs[name]) for name in INPUTS}
    arrays["const_k"], arrays["const_a"], arrays["const_c"] = constants()
    handles = [nc.dram_tensor(f"in_{name}", a.shape, mybir.dt.from_np(a.dtype), kind="ExternalInput").ap() for name, a in arrays.items()]
    out = nc.dram_tensor("out_rows", (NB, T, D), F32, kind="ExternalOutput").ap()
    build(nc, *handles, out)
    r = run_bass_kernel_spmd(nc, [{f"in_{name}": a for name, a in arrays.items()}], core_ids=[0])
    return r.results[0]["out_rows"]
```
